# Optimizing a Trainium2 kernel written in Bass

```python
import numpy as np
import jax
import jax.numpy as jnp

def _softmax(x, axis=-1):
    return jax.nn.softmax(x, axis=axis)

def _gelu(x):
    return jax.nn.gelu(x, approximate=True)

def _silu(x):
    return jax.nn.silu(x)

def _sigmoid(x):
    return jax.nn.sigmoid(x)

def _layernorm(x, axis=-1, eps=1e-05):
    m = jnp.mean(x, axis=axis, keepdims=True)
    v = jnp.var(x, axis=axis, keepdims=True)
    return (x - m) / jnp.sqrt(v + eps)

def _scatter_add(tgt, idx, src, axis=0):
    return tgt.at[idx].add(src)

def _segment_sum(src, seg, n):
    return jax.ops.segment_sum(src, seg, n)
kernel_name = 'mk_decoder_preln_d1_seqx_r4_462381'

def setup_inputs(seed: int=0):
    np.random.seed(seed)
    _w = jnp.asarray

    def _rec_inputs():
        import jax
        import jax.numpy as jnp
        _rk = jax.random.key(seed)
        x = -0.000125 + 0.9999 * jax.random.normal(jax.random.fold_in(_rk, 1), (4, 512, 512), jnp.float32)
        _lenS = 512 - jax.random.randint(jax.random.fold_in(_rk, 7), (4,), 0, max(1, 512 // 4) + 1, jnp.int32)
        _lenS2 = 512 - jax.random.randint(jax.random.fold_in(_rk, 8), (4,), 0, max(1, 512 // 4) + 1, jnp.int32)
        fside_BxS2xS2_0 = -3.05549e-07 + 0.0199987 * jax.random.normal(jax.random.fold_in(_rk, 11), (4, 512, 512), jnp.float32)
        _ctx_1024P = jax.random.normal(jax.random.fold_in(_rk, 12), (4, 16, 256), jnp.float32)
        _ctx_1024c = jax.random.dirichlet(jax.random.fold_in(_rk, 512), 0.3 * jnp.ones((16,), jnp.float32), (4, 512))
        _ctx_1024t = jnp.einsum('bsk,bkd->bsd', _ctx_1024c, _ctx_1024P)
        _ctx_1024t = _ctx_1024t * jax.lax.rsqrt(jnp.mean(jnp.square(_ctx_1024t)) + 1e-12) * 0.953939
        ctx_1024 = 6.82029e-06 + 0.0200006 * (_ctx_1024t + 0.3 * jax.random.normal(jax.random.fold_in(_rk, 612), (4, 512, 256), jnp.float32))
        return (x, fside_BxS2xS2_0, ctx_1024)
    x, fside_BxS2xS2_0, ctx_1024 = _rec_inputs()

    def _L0_attn_setup():
        import jax, jax.numpy as jnp
        import numpy as np
        B_, L_, DM, DI, DS, DTR, DC = (1, 512, 512, 1024, 16, 128, 4)
        key = jax.random.key(seed)
        ks = jax.random.split(key, 8)
        s = lambda k, shape, scale: jax.random.normal(k, shape, jnp.float32) * scale
        inp = {'hidden_states': s(ks[0], (B_, L_, DM), 1.0), 'in_proj_weight': s(ks[1], (2 * DI, DM), DM ** (-0.5)), 'conv1d_weight': s(ks[2], (DI, 1, DC), DC ** (-0.5)), 'x_proj_weight': s(ks[3], (DTR + 2 * DS, DI), DI ** (-0.5)), 'dt_proj_weight': s(ks[4], (DI, DTR), DTR ** (-0.5)), 'out_proj_weight': s(ks[5], (DM, DI), DI ** (-0.5))}
        dt = jnp.exp(jax.random.uniform(ks[6], (DI,), jnp.float32) * (np.log(0.1) - np.log(0.001)) + np.log(0.001))
        dt = jnp.clip(dt, 0.0001, None)
        inp['dt_proj_bias'] = dt + jnp.log(-jnp.expm1(-dt))
        inp['A_log'] = jnp.log(jnp.tile(jnp.arange(1, DS + 1, dtype=jnp.float32), (DI, 1)))
        inp['D'] = jnp.ones((DI,), jnp.float32)
        return inp
    _L0_attn_all = _L0_attn_setup()
    _L0_attn_in = {k: v for k, v in _L0_attn_all.items() if k in ('in_proj_weight', 'conv1d_weight', 'x_proj_weight', 'dt_proj_weight', 'dt_proj_bias', 'A_log', 'D', 'out_proj_weight')}
    del _L0_attn_all

    def _L0_xattn_setup():
        import jax, jax.numpy as jnp
        import numpy as np
        EPS = 1e-06
        QMAX = 127.0

        def _smooth_quant_linear(x, w):
            amax_x = jnp.max(jnp.abs(x), axis=0)
            amax_w = jnp.max(jnp.abs(w), axis=0)
            s = jnp.sqrt(jnp.maximum(amax_x, EPS) / jnp.maximum(amax_w, EPS))
            s = jnp.maximum(s, EPS)
            xs = x / s
            ws = w * s
            x_scale = jnp.maximum(jnp.max(jnp.abs(xs), axis=-1, keepdims=True), EPS) / QMAX
            w_scale = jnp.maximum(jnp.max(jnp.abs(ws), axis=-1, keepdims=True), EPS) / QMAX
            x_q = jnp.clip(jnp.round(xs / x_scale), -QMAX, QMAX)
            w_q = jnp.clip(jnp.round(ws / w_scale), -QMAX, QMAX)
            return x_q @ w_q.T * x_scale * w_scale.T

        def _expert_forward(xe, guw, dw):
            h = _smooth_quant_linear(xe, guw)
            gate, up = jnp.split(h, 2, axis=-1)
            a = jax.nn.silu(gate) * up
            return _smooth_quant_linear(a, dw)
        key = jax.random.key(seed)
        k1, k2, k3 = jax.random.split(key, 3)
        E, T, D, I = (8, 512, 512, 256)
        x = jax.random.normal(k1, (E, T, D), dtype=jnp.float32)
        gate_up_weight = jax.random.normal(k2, (E, 2 * I, D), dtype=jnp.float32) * 0.02
        down_weight = jax.random.normal(k3, (E, D, I), dtype=jnp.float32) * 0.02
        return {'x': x, 'gate_up_weight': gate_up_weight, 'down_weight': down_weight}
    _L0_xattn_all = _L0_xattn_setup()
    _L0_xattn_in = {k: v for k, v in _L0_xattn_all.items() if k in ()}
    del _L0_xattn_all

    def _L0_ffn_setup():
        import jax, jax.numpy as jnp
        import numpy as np
        H = 512
        E = 16
        I = 128
        IS = 512
        TOP_K = 2
        B, S = (1, 512)
        key = jax.random.key(seed)
        ks = jax.random.split(key, 9)
        std = 0.02
        return {'hidden_states': jax.random.normal(ks[0], (B, S, H), dtype=jnp.float32), 'gate_w': jax.random.normal(ks[1], (E, H), dtype=jnp.float32) * std, 'w1': jax.random.normal(ks[2], (E, I, H), dtype=jnp.float32) * std, 'w2': jax.random.normal(ks[3], (E, H, I), dtype=jnp.float32) * std, 'w3': jax.random.normal(ks[4], (E, I, H), dtype=jnp.float32) * std, 'ws_gate': jax.random.normal(ks[5], (IS, H), dtype=jnp.float32) * std, 'ws_up': jax.random.normal(ks[6], (IS, H), dtype=jnp.float32) * std, 'ws_down': jax.random.normal(ks[7], (H, IS), dtype=jnp.float32) * std, 'shared_gate_w': jax.random.normal(ks[8], (1, H), dtype=jnp.float32) * std}
    _L0_ffn_all = _L0_ffn_setup()
    _L0_ffn_in = {k: v for k, v in _L0_ffn_all.items() if k in ('gate_w', 'w1', 'w2', 'w3', 'ws_gate', 'ws_up', 'ws_down', 'shared_gate_w')}
    del _L0_ffn_all
    return {'x': x, 'fside_BxS2xS2_0': fside_BxS2xS2_0, 'ctx_1024': ctx_1024, 'L0_attn_in_proj_weight': _L0_attn_in['in_proj_weight'], 'L0_attn_conv1d_weight': _L0_attn_in['conv1d_weight'], 'L0_attn_x_proj_weight': _L0_attn_in['x_proj_weight'], 'L0_attn_dt_proj_weight': _L0_attn_in['dt_proj_weight'], 'L0_attn_dt_proj_bias': _L0_attn_in['dt_proj_bias'], 'L0_attn_A_log': _L0_attn_in['A_log'], 'L0_attn_D': _L0_attn_in['D'], 'L0_attn_out_proj_weight': _L0_attn_in['out_proj_weight'], 'L0_ffn_gate_w': _L0_ffn_in['gate_w'], 'L0_ffn_w1': _L0_ffn_in['w1'], 'L0_ffn_w2': _L0_ffn_in['w2'], 'L0_ffn_w3': _L0_ffn_in['w3'], 'L0_ffn_ws_gate': _L0_ffn_in['ws_gate'], 'L0_ffn_ws_up': _L0_ffn_in['ws_up'], 'L0_ffn_ws_down': _L0_ffn_in['ws_down'], 'L0_ffn_shared_gate_w': _L0_ffn_in['shared_gate_w']}

def reference(x, fside_BxS2xS2_0, ctx_1024, L0_attn_in_proj_weight, L0_attn_conv1d_weight, L0_attn_x_proj_weight, L0_attn_dt_proj_weight, L0_attn_dt_proj_bias, L0_attn_A_log, L0_attn_D, L0_attn_out_proj_weight, L0_ffn_gate_w, L0_ffn_w1, L0_ffn_w2, L0_ffn_w3, L0_ffn_ws_gate, L0_ffn_ws_up, L0_ffn_ws_down, L0_ffn_shared_gate_w):
    import jax
    import jax.numpy as jnp

    def _L0_attn_ref(hidden_states, in_proj_weight, conv1d_weight, x_proj_weight, dt_proj_weight, dt_proj_bias, A_log, D, out_proj_weight):
        import jax, jax.numpy as jnp
        import numpy as np
        B_, L_, DM, DI, DS, DTR, DC = (1, 512, 512, 1024, 16, 128, 4)
        b, l, dm = hidden_states.shape
        di, ds = A_log.shape
        xz = jnp.einsum('ed,bld->bel', in_proj_weight, hidden_states)
        x, z = (xz[:, :di], xz[:, di:])
        x = jax.lax.conv_general_dilated(x, conv1d_weight, window_strides=(1,), padding=[(DC - 1, 0)], dimension_numbers=('NCH', 'OIH', 'NCH'), feature_group_count=di)
        x = jax.nn.silu(x)
        x_dbl = jnp.einsum('pd,bdl->blp', x_proj_weight, x)
        dt, Bc, Cc = jnp.split(x_dbl, [DTR, DTR + ds], axis=-1)
        delta = jnp.einsum('dr,blr->bld', dt_proj_weight, dt) + dt_proj_bias
        delta = jax.nn.softplus(delta)
        A = -jnp.exp(A_log)
        u = jnp.transpose(x, (0, 2, 1))

        def step(h, inputs):
            d_t, B_t, C_t, u_t = inputs
            dA = jnp.exp(d_t[..., None] * A)
            h = h * dA + (d_t * u_t)[..., None] * B_t[:, None, :]
            y = jnp.einsum('bdn,bn->bd', h, C_t)
            return (h, y)
        h0 = jnp.zeros((b, di, ds), hidden_states.dtype)
        xs = (jnp.swapaxes(delta, 0, 1), jnp.swapaxes(Bc, 0, 1), jnp.swapaxes(Cc, 0, 1), jnp.swapaxes(u, 0, 1))
        _, ys = jax.lax.scan(step, h0, xs)
        y = jnp.swapaxes(ys, 0, 1) + u * D
        y = y * jax.nn.silu(jnp.transpose(z, (0, 2, 1)))
        return jnp.einsum('md,bld->blm', out_proj_weight, y)

    def _L0_xattn_ref(x, gate_up_weight, down_weight):
        import jax, jax.numpy as jnp
        import numpy as np
        EPS = 1e-06
        QMAX = 127.0

        def _smooth_quant_linear(x, w):
            amax_x = jnp.max(jnp.abs(x), axis=0)
            amax_w = jnp.max(jnp.abs(w), axis=0)
            s = jnp.sqrt(jnp.maximum(amax_x, EPS) / jnp.maximum(amax_w, EPS))
            s = jnp.maximum(s, EPS)
            xs = x / s
            ws = w * s
            x_scale = jnp.maximum(jnp.max(jnp.abs(xs), axis=-1, keepdims=True), EPS) / QMAX
            w_scale = jnp.maximum(jnp.max(jnp.abs(ws), axis=-1, keepdims=True), EPS) / QMAX
            x_q = jnp.clip(jnp.round(xs / x_scale), -QMAX, QMAX)
            w_q = jnp.clip(jnp.round(ws / w_scale), -QMAX, QMAX)
            return x_q @ w_q.T * x_scale * w_scale.T

        def _expert_forward(xe, guw, dw):
            h = _smooth_quant_linear(xe, guw)
            gate, up = jnp.split(h, 2, axis=-1)
            a = jax.nn.silu(gate) * up
            return _smooth_quant_linear(a, dw)
        return jax.vmap(_expert_forward)(x, gate_up_weight, down_weight)

    def _L0_ffn_ref(hidden_states, gate_w, w1, w2, w3, ws_gate, ws_up, ws_down, shared_gate_w):
        import jax, jax.numpy as jnp
        import numpy as np
        H = 512
        E = 16
        I = 128
        IS = 512
        TOP_K = 2
        B, S = (1, 512)
        b, s, h = hidden_states.shape
        x = hidden_states.reshape(-1, h)
        T = x.shape[0]
        router_logits = x @ gate_w.T
        routing = jax.nn.softmax(router_logits.astype(jnp.float32), axis=-1)
        topw, sel = jax.lax.top_k(routing, TOP_K)
        topw = topw / jnp.sum(topw, axis=-1, keepdims=True)
        topw = topw.astype(x.dtype)
        combine = jnp.zeros((T, E), dtype=x.dtype).at[jnp.arange(T)[:, None], sel].set(topw)
        hmid = jax.nn.silu(jnp.einsum('th,eih->tei', x, w1)) * jnp.einsum('th,eih->tei', x, w3)
        hmid = hmid * combine[:, :, None]
        moe_out = jnp.einsum('tei,ehi->th', hmid, w2)
        shared = jax.nn.silu(x @ ws_gate.T) * (x @ ws_up.T) @ ws_down.T
        shared = jax.nn.sigmoid(x @ shared_gate_w.T) * shared
        return (moe_out + shared).reshape(b, s, h)
    x = x + _L0_attn_ref(_layernorm(x, axis=-1), L0_attn_in_proj_weight, L0_attn_conv1d_weight, L0_attn_x_proj_weight, L0_attn_dt_proj_weight, L0_attn_dt_proj_bias, L0_attn_A_log, L0_attn_D, L0_attn_out_proj_weight)
    x = x + _L0_xattn_ref(_layernorm(x, axis=-1), fside_BxS2xS2_0, ctx_1024)
    x = x + _L0_ffn_ref(_layernorm(x, axis=-1), L0_ffn_gate_w, L0_ffn_w1, L0_ffn_w2, L0_ffn_w3, L0_ffn_ws_gate, L0_ffn_ws_up, L0_ffn_ws_down, L0_ffn_shared_gate_w)
    return x

_drawn_inputs = setup_inputs


def setup_inputs(seed=0):
    import zlib

    import numpy as np

    out = dict(_drawn_inputs(seed))
    spreads = {'L0_attn_D': (1.0, 0.2)}
    factors = {'L0_ffn_gate_w': 3.908,
     'L0_ffn_w1': 3.723,
     'L0_ffn_w2': 3.655,
     'L0_ffn_w3': 3.647,
     'L0_ffn_shared_gate_w': 38.807,
     'L0_ffn_ws_gate': 2.945,
     'L0_ffn_ws_up': 2.902,
     'L0_ffn_ws_down': 2.892}
    for name, (base, spread) in spreads.items():
        noise = np.random.default_rng([zlib.crc32(name.encode()), seed]).standard_normal(out[name].shape)
        drawn = base * np.exp(spread * noise) if base else spread * noise
        out[name] = jnp.asarray(drawn.astype(out[name].dtype))
    for name, factor in factors.items():
        out[name] = (out[name] * factor).astype(out[name].dtype)
    return out
```

```python
from contextlib import ExitStack

import numpy as np

import concourse.bass as bass
from concourse import mybir

F32 = mybir.dt.float32
BF16 = mybir.dt.bfloat16
U32 = mybir.dt.uint32
ALU = mybir.AluOpType
ACT = mybir.ActivationFunctionType
AX = mybir.AxisListType

P = 128
B = 4
T = 512
D = 512
DI = 1024
NS = 16
DTR = 128
TAPS = 4
INT = 256
NE = 16
NSH = 4
TT = T // P
KD = D // P
NBLK = DI // P
QUARTERS = 4
BLK_Q = NBLK // QUARTERS
EXP_Q = (NE + NSH) // QUARTERS
CN = 2
CHUNKS = NS // CN
CH_Q = BLK_Q * CHUNKS
W_RING = 4
SLOT = [0, 1, 0, 1, 2]
SLOT_USES = [SLOT.count(s) for s in range(3)]
EW = 2 * D + D
EPS_LN = 1e-5
EPS_Q = 1e-6
QMAX = 127.0
MAGIC = 1.5 * 2.0 ** 23
CREDIT = 2
ONE = 1
DOWN_CREDIT = EXP_Q

ITEMS = ([("xi", m) for m in range(8)] + [("z", 0), ("z", 1), ("bc", 0), ("dt", 0), ("z", 2), ("z", 3)]
         + [("dl", j) for j in range(8)] + [("z", m) for m in range(4, 8)])
W_ITEMS = [it for it in ITEMS if it[0] in ("xi", "z")]
W_USES = len(W_ITEMS) + NBLK
PHASES = [("g", 0), ("u", 0)]
for _i in range(1, EXP_Q):
    PHASES += [("g", _i), ("u", _i), ("d", _i - 1)]
PHASES += [("d", EXP_Q - 1)]
TH_ORDER = [("xi", m) for m in range(8)] + [("z", m) for m in range(8)]
LINKS = {}
LINKS.update({"A": 42, "LN": 8, "X0": 41, "X1": 31, "G": 24})


def build(nc, x, w_in, conv_w, xp_w, dt_w, dt_b, a_log, d_skip, out_w, gu_w, gu_wT, dn_w, dn_wT, gate_w,
          exp_w, out):
    with ExitStack() as ctx:
        def sb(name, shape, dt=F32):
            return ctx.enter_context(nc.sbuf_tensor(name, shape, dt))

        def sem(name):
            return ctx.enter_context(nc.semaphore(name))

        bc_dram = nc.dram_tensor("bc_dram", (2 * NS, T), F32, kind="Internal").ap()
        comb_dram = nc.dram_tensor("comb_dram", (NE + 1, T), F32, kind="Internal").ap()

        ident = sb("ident", [P, P])
        identb = sb("identb", [P, P], BF16)
        ones = sb("ones", [P, P])
        zerob = sb("zerob", [P, P], BF16)
        magic = sb("magic", [P, 1])
        halfpow = sb("halfpow", [P, 2, TT])
        iota = sb("iota", [P, NE])
        A_sb = sb("A_sb", [P, NBLK, NS])
        cw = sb("cw", [P, NBLK, TAPS])
        dtb = sb("dtb", [P, NBLK])
        dsk = sb("dsk", [P, NBLK])
        xpw = sb("xpw", [P, NBLK, DTR + 2 * NS])
        dtw = sb("dtw", [P, DI])
        gatew = sb("gatew", [P, KD, NE + 1])
        wst = sb("wst", [P, W_RING, 512])
        ew = sb("ew", [P, 3, EW])
        comb_bc = sb("comb_bc", [P, 3, T])
        x2 = sb("x2", [P, TT, D])
        x3T = sb("x3T", [P, KD, T])
        delta = sb("delta", [P, NBLK, T])
        u = sb("u", [P, NBLK, T])
        zg = sb("zg", [P, NBLK, T])
        BB = sb("BB", [P, NS, T])
        CB = sb("CB", [P, NS, T])
        du = sb("du", [P, 1, T])
        work = sb("work", [P, 6144])
        etm = sb("etm", [P, 2, T])
        hm = sb("hm", [P, 2, T])
        st = sb("st", [P, TT, 6])
        mv = sb("mv", [P, TT, 2])
        rstd = sb("rstd", [P, TT])
        col = sb("col", [P, 8, 4])
        rr = sb("rr", [P, 3, 2 * TT])
        dtT = hm[:, 0, :]
        bcS = hm[0:2 * NS, 1, :]

        dA = work[:, 0:2048].rearrange("p (s n t) -> p s n t", s=2, n=CN)
        dBu = work[:, 2048:4096].rearrange("p (s n t) -> p s n t", s=2, n=CN)
        h = work[:, 4096:6144].rearrange("p (s n t) -> p s n t", s=2, n=CN)
        xpad = work[:, 0:1030].rearrange("p (s t) -> p s t", s=2)
        xT = work[:, 2048:4096].rearrange("p (k t) -> p k t", k=KD)
        xn = work[:, 4096:6144].rearrange("p (k t) -> p k t", k=TT)
        wsc = work[:, 0:512]
        lg = work[:, 0:68].rearrange("p (t e) -> p t e", t=TT)
        comb = work[:, 68:136].rearrange("p (t e) -> p t e", t=TT)
        pr = work[:, 136:328].rearrange("p (i t e) -> p i t e", i=3, t=TT)
        top = work[:, 328:360].rearrange("p (t e) -> p t e", t=TT)
        topi = work[:, 360:392].bitcast(U32).rearrange("p (t e) -> p t e", t=TT)
        topf = work[:, 392:408].rearrange("p (i t e) -> p i t e", i=2, t=TT)
        gm = work[:, 408:432].rearrange("p (i t) -> p i t", i=6)
        sp_e, sp_err, sp_ln, sp_inv = (
            [work[:, o + i * T:o + (i + 1) * T] for o in (4096, 0)] for i in range(4))
        cT = work[0:NE + 1, 1536:2048]
        hth = work[:, 512:1536].rearrange("p (t i) -> p t i", t=TT)
        dg = work[:, 2048:3072].rearrange("p (k c) -> p k c", k=8)
        act = work[:, 3072:4096].rearrange("p (t i) -> p t i", t=TT)
        guw = delta[:, 0:4, :]
        guwT = delta[:, 4:8, :]
        dnw = u[:, 0:2, :].rearrange("p a (b i) -> p (a b) i", b=2)
        dnwT = u[:, 2:4, :]
        zb = zg[:, :, :].rearrange("p a b -> p (a b)").bitcast(BF16)
        q_rows = [zb[:, 0:2048], zb[:, 2048:4096]]
        q_cols = [zb[:, 4096:6144], zb[:, 6144:8192]]

        bank = [ctx.enter_context(nc.psum_tensor(f"bank{i}", [P, 512], F32)) for i in range(8)]
        bankb = [t[:, :].bitcast(BF16) for t in bank]
        acc = bank[0:4]
        G, U = bank[4], bank[5]
        Y = [bank[6], bank[7]]

        S = {n: sem(n) for n in (
            "const_in zero_done ident_done const_done a_exp x_in x_res var_ready rstd_ready xn_ready tr_done xT_ready a_ps "
            "xpad_ready conv_done th_ready u_ready z_ready bc_ready bc_out dt_ready delta_ready "
            "du_ready dbu_ready da_ready scan_done prod_done hs_ready nsum_done y_done "
            "g_done u_done eth_ready t1_done t2_done hm_ready down_done moe_done fin_done out_done "
            "o_used xw_in xc_ps s_arg s_pow diag_ready sbc_ps rinv_ready wdiag_ready mg_ready wsc_ps "
            "wsc_ready q_ready qT_ps qT_ready lin_ps h_ready hth_ready a_ready x3_ready lg_ps ex_arg "
            "ex_ready comb_ready comb_ps cT_ready comb_out init linkA linkLN linkX linkG linkO linkS linkSP sp_e_ready relu_ready sp_inv_ready sp_err_ready sum_ready").split()}
        w_in_s = [sem(f"w_in{i}") for i in range(W_RING)]
        ew_in = [sem(f"ew_in{i}") for i in range(3)]
        bcast = [sem(f"bcast{i}") for i in range(4)]

        def wait(eng, name, value):
            s = S[name] if isinstance(name, str) else name
            if not isinstance(value, int) or value > 0:
                eng.wait_ge(s, value)

        class Chain:

            def __init__(self, eng, name, base):
                self.eng, self.sem, self.base, self.n = eng, S[name], base, 0

            def mark(self, ins):
                self.n += 1
                ins.then_inc(self.sem, 1)

            def wait(self):
                self.eng.wait_ge(self.sem, self.base + self.n)

            def __call__(self, ins):
                self.mark(ins)
                self.wait()

        block = ctx.enter_context(nc.Block())

        @block.sync
        def _(sp):
            for dst, src in ((cw, conv_w), (dtb, dt_b), (dsk, d_skip), (A_sb, a_log), (xpw, xp_w),
                             (dtw, dt_w), (gatew, gate_w)):
                sp.dma_start(dst[:], src).then_inc(S["const_in"], 16)

            def batch_x(b):
                return x[bass.ds(b, 1), :, :].rearrange("o (t p) d -> p (o t) d", p=P)

            def weight(b, n, src):
                m = n - W_RING
                if m < 0:
                    wait(sp, "o_used", NBLK * b + m + 1)
                elif m < len(W_ITEMS):
                    sp.wait_ge(S["a_ps"], len(ITEMS) * b + ITEMS.index(W_ITEMS[m]) + 1)
                else:
                    sp.wait_ge(S["o_used"], NBLK * b + m - len(W_ITEMS) + 1)
                sp.dma_start(wst[:, n % W_RING, :], src).then_inc(w_in_s[n % W_RING], 16)

            def load_a(b):
                wait(sp, "tr_done", 3 * b)
                sp.dma_start(xn, batch_x(b)).then_inc(S["x_in"], 16)
                n = 0
                for kind, m in ITEMS:
                    if kind in ("xi", "z"):
                        weight(b, n, w_in[m + (NBLK if kind == "z" else 0)])
                        n += 1
                    if (kind, m) == ("z", 3):
                        sp.wait_ge(S["bc_ready"], 1 + b)
                        sp.dma_start(bc_dram, bcS).then_inc(S["bc_out"], 16)
                        sp.wait_ge(S["bc_out"], 16 * b + 16)
                        for g in range(4):
                            for half, dst in enumerate((BB, CB)):
                                rows = bc_dram[half * NS + 4 * g:half * NS + 4 * g + 4, :]
                                sp.dma_start(dst[:, 4 * g:4 * g + 4, :],
                                             rows.rearrange("n t -> (n t)").partition_broadcast(P)
                                             .rearrange("p (n t) -> p n t", n=4)).then_inc(bcast[g], 16)

            def load_e(be, jj):
                qe = 4 * be + jj
                sp.wait_ge(S["comb_out"], 16 * be + 16)
                prev = [3, 4, 1 + DOWN_CREDIT, 2 + DOWN_CREDIT, 5]
                for i in range(EXP_Q):
                    sp.wait_ge(S["down_done"], EXP_Q * qe + prev[i])
                    if i < EXP_Q - 1:
                        e, row = jj * (EXP_Q - 1) + i, jj * (EXP_Q - 1) + i
                    else:
                        e, row = jj + NE, NE
                    sp.dma_start(ew[:, SLOT[i], :], exp_w[bass.ds(e, 1), :, :].rearrange("o p n -> p (o n)")
                                 ).then_inc(ew_in[SLOT[i]], 16)
                    src = comb_dram[bass.ds(row, 1), :] if i < EXP_Q - 1 else comb_dram[NE:NE + 1, :]
                    sp.dma_start(comb_bc[:, SLOT[i], :], src.rearrange("o t -> (o t)").partition_broadcast(P)
                                 ).then_inc(ew_in[SLOT[i]], 16)

            def load_o(b):
                sp.wait_ge(S["nsum_done"], CREDIT + 4 * CH_Q * (b + 1))
                sp.dma_start(xn, batch_x(b)).then_inc(S["x_res"], 16)
                for k in range(NBLK):
                    weight(b, len(W_ITEMS) + k, out_w[k])
                sp.wait_ge(S["y_done"], CREDIT + NBLK * (b + 1))
                for dst, src in ((guw, gu_w), (guwT, gu_wT), (dnw, dn_w), (dnwT, dn_wT)):
                    sp.dma_start(dst, src[bass.ds(b, 1)].rearrange("o p k n -> p (o k) n")
                                 ).then_inc(S["xw_in"], 16)

            def store(be):
                sp.wait_ge(S["fin_done"], TT * be + TT)
                sp.dma_start(out[bass.ds(be, 1), :, :].rearrange("o (t p) d -> p (o t) d", p=P), x2[:]
                             ).then_inc(S["out_done"], 16)

            def comb_rows(b):
                sp.wait_ge(S["cT_ready"], b + 1)
                sp.dma_start(comb_dram, cT).then_inc(S["comb_out"], 16)

            load_a(0)
            load_o(0)
            comb_rows(0)
            with sp.Fori(1, B) as b:
                load_a(b)
                with sp.Fori(0, QUARTERS) as jj:
                    load_e(b - 1, jj)
                store(b - 1)
                load_o(b)
                comb_rows(b)
            with sp.Fori(0, QUARTERS) as jj:
                load_e(B - 1, jj)
            store(B - 1)
            sp.wait_ge(S["out_done"], 16 * B)

        @block.gpsimd
        def _(pool):
            nc.gpsimd.memset(ident[:], 0.0).then_inc(S["zero_done"], 1)
            nc.gpsimd.memset(ones[:], 1.0)
            nc.gpsimd.memset(zerob[:], 0.0)
            nc.gpsimd.memset(magic[:], MAGIC)
            nc.gpsimd.memset(halfpow[:, 0, :], 0.5)
            nc.gpsimd.memset(halfpow[:, 1, :], -0.5).then_inc(S["ident_done"], 1)
            pool.wait_ge(S["zero_done"], 1)
            nc.gpsimd.affine_select(out=ident[:], in_=ident[:], compare_op=ALU.not_equal, fill=1.0, base=0,
                                    pattern=[[-1, P]], channel_multiplier=1).then_inc(S["ident_done"], 1)
            pool.wait_ge(S["ident_done"], 2)
            nc.gpsimd.tensor_copy(identb[:], ident[:]).then_inc(S["const_done"], 1)
            nc.gpsimd.iota(iota[:], pattern=[[1, NE]], base=0, channel_multiplier=0,
                           allow_small_or_imprecise_dtypes=True).then_inc(S["const_done"], 1)

            def power(ready, value, dst, src, exponent, done):
                pool.wait_ge(S[ready], value)
                nc.gpsimd.tensor_tensor(dst, src, exponent, ALU.pow).then_inc(S[done], 1)

            def norm(l):
                power("var_ready", l + 1, rstd[:], mv[:, :, 1], halfpow[:, 1, :], "rstd_ready")

            def step(b, jj, scan, experts):
                q = 4 * b + jj
                qe = 4 * (b - 1) + jj
                if scan:
                    pool.wait_ge(S["delta_ready"], NBLK * (b + 1))
                    pool.wait_ge(S["u_ready"], NBLK * (b + 1))
                    pool.wait_ge(S["a_ps"], len(ITEMS) * (b + 1))

                def chunk(c):
                    jl, s, n0 = c // CHUNKS, c % 2, CN * (c % CHUNKS)
                    if c % CHUNKS == 0:
                        dj = delta[:, bass.ds(jj * BLK_Q + jl, 1), :].rearrange("p o t -> p (o t)")
                        uj = u[:, bass.ds(jj * BLK_Q + jl, 1), :].rearrange("p o t -> p (o t)")
                        pool.wait_ge(S["dbu_ready"], ONE + CH_Q * q + c)
                        nc.gpsimd.tensor_tensor(du[:, 0, :], dj, uj, ALU.mult).then_inc(S["du_ready"], 1)
                        pool.wait_ge(S["du_ready"], BLK_Q * q + jl + 1)
                    pool.wait_ge(bcast[n0 // 4], 32 * (b + 1))
                    pool.wait_ge(S["scan_done"], CREDIT + CH_Q * q + c - 1)
                    nc.gpsimd.tensor_tensor(
                        dBu[:, s, :, :], du[:, 0:1, :].broadcast_to([P, CN, T]),
                        BB[:, n0:n0 + CN, :], ALU.mult).then_inc(S["dbu_ready"], 1)

                def gate(i):
                    prev = [0, 4 - DOWN_CREDIT, 1, 2, 3]
                    pool.wait_ge(S["t2_done"], ONE + EXP_Q * qe + i + 1)
                    pool.wait_ge(S["down_done"], DOWN_CREDIT + EXP_Q * qe + prev[i])
                    pool.wait_ge(ew_in[SLOT[i]], 32 * (SLOT_USES[SLOT[i]] * qe + SLOT[:i + 1].count(SLOT[i])))
                    nc.gpsimd.tensor_tensor(hm[:, i % 2, :], etm[:, 1, :], comb_bc[:, SLOT[i], :],
                                            ALU.mult).then_inc(S["hm_ready"], 1)

                for p in range(CH_Q):
                    if scan:
                        chunk(p)
                    if experts and p - 2 >= 0 and ("u", p - 2) and p - 2 < len(PHASES) and PHASES[p - 2][0] == "u":
                        gate(PHASES[p - 2][1])

            def softplus(b):
                for m in range(NBLK):
                    pool.wait_ge(S["sp_inv_ready"], NBLK * b + m + 1)
                    nc.gpsimd.tensor_tensor(delta[:, m, :], delta[:, m, :], sp_ln[m % 2], ALU.add
                                            ).then_inc(S["sum_ready"], 1)
                    pool.wait_ge(S["sum_ready"], NBLK * b + m + 1)
                    pool.wait_ge(S["sp_err_ready"], NBLK * b + m + 1)
                    nc.gpsimd.tensor_tensor(delta[:, m, :], delta[:, m, :], sp_err[m % 2], ALU.subtract
                                            ).then_inc(S["delta_ready"], 1)

            def batch_tail(b):
                norm(3 * b + 1)
                for layer in range(2):
                    power("s_arg", 2 * b + layer + 1, col[:, 4, 0:(KD, 2)[layer]], col[:, 3, 0:(KD, 2)[layer]],
                          halfpow[:, 0, 0:(KD, 2)[layer]], "s_pow")
                norm(3 * b + 2)

            norm(0)
            softplus(0)
            with pool.Fori(0, QUARTERS) as jj:
                step(0, jj, True, False)
            batch_tail(0)
            with pool.Fori(1, B) as b:
                norm(3 * b)
                softplus(b)
                with pool.Fori(0, QUARTERS) as jj:
                    step(b, jj, True, True)
                batch_tail(b)
            with pool.Fori(0, QUARTERS) as jj:
                step(B, jj, False, True)

        @block.scalar
        def _(sc):
            sc.wait_ge(S["const_in"], 16 * 7)
            nc.scalar.activation(A_sb[:], A_sb[:], ACT.Exp).then_inc(S["a_exp"], 1)

            def stage_a(b):
                sc.wait_ge(S["tr_done"], 3 * b + 1)
                for k in range(2):
                    nc.scalar.copy(xT[:, k, :], acc[k][:, :]).then_inc(S["xT_ready"], 1)

                def tanh_x(m):
                    r = m
                    sc.wait_ge(S["conv_done"], NBLK * b + m + 1)
                    if r >= 2:
                        sc.wait_ge(S["u_ready"], NBLK * b + r - 1)
                    nc.scalar.activation(etm[:, r % 2, :], u[:, m, :], ACT.Tanh).then_inc(S["th_ready"], 1)

                for n, (kind, m) in enumerate(ITEMS):
                    sc.wait_ge(S["a_ps"], len(ITEMS) * b + n + 1)
                    ps = bank[4 + n % 4]
                    if kind == "xi":
                        if m >= 2:
                            sc.wait_ge(S["conv_done"], NBLK * b + m - 1)
                        nc.scalar.copy(xpad[:, m % 2, TAPS - 1:TAPS - 1 + T], ps[:, :]).then_inc(S["xpad_ready"], 1)
                        if m >= 1:
                            tanh_x(m - 1)
                    elif kind == "z":
                        if m == 0:
                            tanh_x(NBLK - 1)
                            sc.wait_ge(S["u_ready"], NBLK * b + NBLK - 1)
                        elif m == 1:
                            sc.wait_ge(S["u_ready"], NBLK * b + NBLK)
                        else:
                            sc.wait_ge(S["z_ready"], NBLK * b + m - 1)
                        nc.scalar.activation(etm[:, m % 2, :], ps[:, :], ACT.Tanh, scale=0.5
                                             ).then_inc(S["th_ready"], 1)
                    elif kind == "bc":
                        nc.scalar.copy(bcS, ps[0:2 * NS, :]).then_inc(S["bc_ready"], 1)
                    elif kind == "dt":
                        nc.scalar.copy(dtT, ps[:, :]).then_inc(S["dt_ready"], 1)
                    else:
                        s = m % 2
                        if m < 2:
                            sc.wait_ge(S["conv_done"], NBLK * (b + 1))
                        else:
                            sc.wait_ge(S["delta_ready"], NBLK * b + m - 1)
                        nc.scalar.activation(sp_e[s], ps[:, :], ACT.Abs, bias=dtb[:, m:m + 1]
                                             ).then_inc(S["linkSP"], 1)
                        sc.wait_ge(S["linkSP"], 2 * (NBLK * b + m) + 1)
                        nc.scalar.activation(sp_e[s], sp_e[s], ACT.Exp, scale=-1.0).then_inc(S["sp_e_ready"], 1)
                        sc.wait_ge(S["sp_e_ready"], NBLK * b + m + 1)
                        nc.scalar.activation(sp_ln[s], sp_e[s], ACT.Ln, bias=ones[:, 0:1]).then_inc(S["linkSP"], 1)
                        nc.scalar.activation(delta[:, m, :], ps[:, :], ACT.Relu, bias=dtb[:, m:m + 1]
                                             ).then_inc(S["relu_ready"], 1)
                        sc.wait_ge(S["linkSP"], 2 * (NBLK * b + m) + 2)
                        nc.scalar.activation(sp_inv[s], sp_ln[s], ACT.Exp, scale=-1.0
                                             ).then_inc(S["sp_inv_ready"], 1)

            def step(b, jj, scan, experts):
                q = 4 * b + jj
                qe = 4 * (b - 1) + jj
                if scan:
                    sc.wait_ge(S["delta_ready"], NBLK * (b + 1))

                def chunk(c):
                    jl, s, n0 = c // CHUNKS, c % 2, CN * (c % CHUNKS)
                    dj = delta[:, bass.ds(jj * BLK_Q + jl, 1), 1:T].rearrange("p o t -> p (o t)")
                    sc.wait_ge(S["scan_done"], CREDIT + CH_Q * q + c - 1)
                    for i in range(CN):
                        a = A_sb[:, bass.ds(jj * BLK_Q + jl, 1), n0 + i:n0 + i + 1].rearrange("p o n -> p (o n)")
                        ins = nc.scalar.activation(dA[:, s, i, 1:T], dj, ACT.Exp, scale=a)
                    ins.then_inc(S["da_ready"], 1)

                def tanh_g(i):
                    sc.wait_ge(S["g_done"], EXP_Q * qe + i + 1)
                    sc.wait_ge(S["t1_done"], ONE + EXP_Q * qe + i)
                    nc.scalar.activation(etm[:, 0, :], G[:, :], ACT.Tanh, scale=0.5).then_inc(S["eth_ready"], 1)

                for p in range(CH_Q):
                    if scan:
                        chunk(p)
                    if experts and p >= 1 and p - 1 < len(PHASES) and PHASES[p - 1][0] == "g":
                        tanh_g(PHASES[p - 1][1])

            def quant(b, layer, src_x, src_w):
                r = 2 * b + layer
                sc.wait_ge(S["rinv_ready"], r + 1)
                for i in range(2 * TT):
                    src = (src_x if i < TT else src_w)[:, i % TT, :]
                    nc.scalar.activation(src, src, ACT.Identity, scale=rr[:, 2, i:i + 1], bias=magic[:, 0:1]
                                         ).then_inc(S["mg_ready"], 1)
                sc.wait_ge(S["wsc_ps"], r + 1)
                nc.scalar.copy(wsc, bank[6][:, :]).then_inc(S["wsc_ready"], 1)

            def batch_tail(b):
                quant(b, 0, xn, guw)
                for t in range(TT):
                    sc.wait_ge(S["h_ready"], TT * b + t + 1)
                    nc.scalar.activation(hth[:, t, :], xn[:, t, 0:INT], ACT.Tanh, scale=0.5
                                         ).then_inc(S["hth_ready"], 1)
                quant(b, 1, act, dnw)
                sc.wait_ge(S["tr_done"], 3 * b + 3)
                for k in range(KD):
                    nc.scalar.copy(x3T[:, k, :], acc[k][:, :]).then_inc(S["x3_ready"], 1)
                sc.wait_ge(S["ex_arg"], b + 1)
                nc.scalar.activation(pr[:, 0, :, :], pr[:, 0, :, :], ACT.Exp)
                nc.scalar.activation(gm[:, 3, :], lg[:, :, NE], ACT.Exp, scale=-1.0).then_inc(S["ex_ready"], 1)
                sc.wait_ge(S["comb_ps"], b + 1)
                nc.scalar.copy(cT, bank[5][0:NE + 1, :]).then_inc(S["cT_ready"], 1)

            stage_a(0)
            with sc.Fori(0, QUARTERS) as jj:
                step(0, jj, True, False)
            batch_tail(0)
            with sc.Fori(1, B) as b:
                stage_a(b)
                with sc.Fori(0, QUARTERS) as jj:
                    step(b, jj, True, True)
                batch_tail(b)
            with sc.Fori(0, QUARTERS) as jj:
                step(B, jj, False, True)

        @block.vector
        def _(ve):
            V = nc.vector
            for i, (free, n) in enumerate((("scan_done", CREDIT), ("nsum_done", CREDIT), ("y_done", CREDIT),
                                           ("t1_done", ONE), ("t2_done", ONE), ("hm_ready", ONE),
                                           ("dbu_ready", ONE), ("down_done", DOWN_CREDIT))):
                V.memset(comb_bc[:, 0, i:i + 1], 0.0).then_inc(S[free], n)
            ve.wait_ge(S["const_in"], 16 * 7)
            V.tensor_scalar(cw[:], cw[:], 0.5, None, ALU.mult).then_inc(S["init"], 1)
            ve.wait_ge(S["a_exp"], 1)
            V.tensor_scalar(A_sb[:], A_sb[:], -1.0, None, ALU.mult).then_inc(S["init"], 1)
            ve.wait_ge(S["init"], 2)
            ve.wait_ge(S["const_done"], 2)

            def carrier():
                V.memset(rr[:, 0, 0:1], 0.0)

            def norm(l, src):
                link = Chain(ve, "linkLN", LINKS["LN"] * l)
                for t in range(TT):
                    link.mark(V.bn_stats(st[:, t, :], src[:, t, :]))
                link.wait()
                carrier()
                for t in range(TT):
                    link.mark(V.bn_aggr(mv[:, t, :], st[:, t, :]))
                link.wait()
                V.tensor_scalar(mv[:, :, 1], mv[:, :, 1], EPS_LN, None, ALU.add).then_inc(S["var_ready"], 1)
                ve.wait_ge(S["rstd_ready"], l + 1)
                ve.wait_ge(S["var_ready"], l + 1)
                for t in range(TT):
                    V.tensor_scalar(xn[:, t, :], src[:, t, :], mv[:, t, 0:1], rstd[:, t:t + 1],
                                    ALU.subtract, ALU.mult).then_inc(S["xn_ready"], 1)
                assert link.n == LINKS["LN"], ("LN", link.n)

            def stage_a(b):
                link = Chain(ve, "linkA", LINKS["A"] * b)
                ve.wait_ge(S["x_in"], 16 * (b + 1))
                norm(3 * b, xn)
                link(V.memset(xpad[:, :, 0:TAPS - 1], 0.0))
                ve.wait_ge(S["tr_done"], 3 * b + 1)
                for k in range(2, KD):
                    V.tensor_copy(xT[:, k, :], acc[k][:, :]).then_inc(S["xT_ready"], 1)

                def conv(m):
                    xp = xpad[:, m % 2, :]
                    ve.wait_ge(S["xpad_ready"], NBLK * b + m + 1)
                    link(V.tensor_scalar(u[:, m, :], xp[:, 0:T], cw[:, m, 0:1], None, ALU.mult))
                    for j in range(1, TAPS):
                        ins = V.scalar_tensor_tensor(out=u[:, m, :], in0=xp[:, j:j + T], scalar=cw[:, m, j:j + 1],
                                                     in1=u[:, m, :], op0=ALU.mult, op1=ALU.add)
                        if j < TAPS - 1:
                            link(ins)
                    ins.then_inc(S["conv_done"], 1)

                def silu_x(m):
                    ve.wait_ge(S["th_ready"], 2 * NBLK * b + m + 1)
                    V.scalar_tensor_tensor(out=u[:, m, :], in0=etm[:, m % 2, :], scalar=1.0, in1=u[:, m, :],
                                           op0=ALU.add, op1=ALU.mult).then_inc(S["u_ready"], 1)

                def silu_z(m, n):
                    ve.wait_ge(S["th_ready"], 2 * NBLK * b + NBLK + m + 1)
                    V.scalar_tensor_tensor(out=zg[:, m, :], in0=etm[:, m % 2, :], scalar=1.0,
                                           in1=bank[4 + n % 4][:, :], op0=ALU.add, op1=ALU.mult
                                           ).then_inc(S["z_ready"], 1)

                def softplus(m):
                    s = m % 2
                    ve.wait_ge(S["sp_e_ready"], NBLK * b + m + 1)
                    link(V.tensor_scalar(sp_err[s], sp_e[s], 1.0, -1.0, ALU.add, ALU.add))
                    link(V.tensor_tensor(sp_err[s], sp_err[s], sp_e[s], ALU.subtract))
                    ve.wait_ge(S["sp_inv_ready"], NBLK * b + m + 1)
                    V.tensor_tensor(sp_err[s], sp_err[s], sp_inv[s], ALU.mult).then_inc(S["sp_err_ready"], 1)

                for n, (kind, m) in enumerate(ITEMS):
                    if kind == "xi":
                        conv(m)
                        if m >= 1:
                            silu_x(m - 1)
                    elif kind == "z":
                        if m == 0:
                            silu_x(NBLK - 1)
                        silu_z(m, n)
                    elif kind == "dl":
                        softplus(m)
                ve.wait_ge(S["delta_ready"], NBLK * (b + 1))
                link.mark(V.memset(dA[:, :, :, 0:1], 0.0))
                assert link.n == LINKS["A"], ("A", link.n)

            def step(b, jj, scan, experts):
                q = 4 * b + jj
                qe = 4 * (b - 1) + jj

                if scan:
                    ve.wait_ge(S["linkA"], LINKS["A"] * (b + 1))

                def scan_chunk(c):
                    s = c % 2
                    ve.wait_ge(S["da_ready"], CH_Q * q + c + 1)
                    ve.wait_ge(S["dbu_ready"], ONE + CH_Q * q + c + 1)
                    ve.wait_ge(S["nsum_done"], CREDIT + CH_Q * q + c - 1)
                    V.tensor_tensor_scan(h[:, s, :, :].rearrange("p n t -> p (n t)"),
                                         dA[:, s, :, :].rearrange("p n t -> p (n t)"),
                                         dBu[:, s, :, :].rearrange("p n t -> p (n t)"),
                                         0.0, ALU.mult, ALU.add).then_inc(S["scan_done"], 1)

                def product(c):
                    s, n0 = c % 2, CN * (c % CHUNKS)
                    ve.wait_ge(S["scan_done"], CREDIT + CH_Q * q + c + 1)
                    ve.wait_ge(bcast[n0 // 4], 32 * (b + 1))
                    V.tensor_tensor(h[:, s, :, :], h[:, s, :, :], CB[:, n0:n0 + CN, :], ALU.mult
                                    ).then_inc(S["prod_done"], 1)

                def pair_sum(c):
                    s = c % 2
                    ve.wait_ge(S["prod_done"], CH_Q * q + c + 1)
                    V.tensor_tensor(h[:, s, 0, :], h[:, s, 0, :], h[:, s, 1, :], ALU.add
                                    ).then_inc(S["hs_ready"], 1)

                def gated(jl):
                    ujl = u[:, bass.ds(jj * BLK_Q + jl, 1), :].rearrange("p o t -> p (o t)")
                    zjl = zg[:, bass.ds(jj * BLK_Q + jl, 1), :].rearrange("p o t -> p (o t)")
                    djl = dsk[:, bass.ds(jj * BLK_Q + jl, 1)]
                    ve.wait_ge(S["nsum_done"], CREDIT + CH_Q * q + CHUNKS * (jl + 1))
                    V.scalar_tensor_tensor(out=ujl, in0=ujl, scalar=djl, in1=Y[jl][:, :], op0=ALU.mult,
                                           op1=ALU.add).then_inc(S["linkS"], 1)
                    ve.wait_ge(S["linkS"], BLK_Q * q + jl + 1)
                    V.scalar_tensor_tensor(out=zjl, in0=ujl, scalar=0.5, in1=zjl, op0=ALU.mult, op1=ALU.mult
                                           ).then_inc(S["y_done"], 1)

                def expert_gate(i):
                    ve.wait_ge(S["eth_ready"], EXP_Q * qe + i + 1)
                    ve.wait_ge(S["hm_ready"], ONE + EXP_Q * qe + i)
                    V.scalar_tensor_tensor(out=etm[:, 1, :], in0=etm[:, 0, :], scalar=1.0, in1=G[:, :],
                                           op0=ALU.add, op1=ALU.mult).then_inc(S["t1_done"], 1)

                def expert_up(i):
                    ve.wait_ge(S["u_done"], EXP_Q * qe + i + 1)
                    ve.wait_ge(S["t1_done"], ONE + EXP_Q * qe + i + 1)
                    V.tensor_tensor(etm[:, 1, :], etm[:, 1, :], U[:, :], ALU.mult).then_inc(S["t2_done"], 1)

                for p in range(CH_Q + 1):
                    if scan:
                        if p < CH_Q:
                            scan_chunk(p)
                        if p >= 1:
                            pair_sum(p - 1)
                        if p < CH_Q:
                            product(p)
                        if p == CHUNKS + 1:
                            gated(0)
                        if p == CH_Q:
                            gated(1)
                    if experts:
                        if 2 <= p < len(PHASES) + 2 and PHASES[p - 2][0] == "g":
                            expert_gate(PHASES[p - 2][1])
                        if 2 <= p < len(PHASES) + 2 and PHASES[p - 2][0] == "u":
                            expert_up(PHASES[p - 2][1])

            def finish(be):
                ve.wait_ge(S["moe_done"], be + 1)
                for t in range(TT):
                    V.tensor_tensor(x2[:, t, :], x2[:, t, :], acc[t][:, :], ALU.add).then_inc(S["fin_done"], 1)

            def quant(b, layer, src_x, src_w, wT, width, skip):
                r = 2 * b + layer
                kt = width // P
                link = Chain(ve, "linkX", (LINKS["X0"] + LINKS["X1"]) * b + (LINKS["X0"] if layer else 0))
                ve.wait_ge(S["xw_in"], 64 * (b + 1))
                for k in range(kt):
                    link(V.tensor_reduce(col[:, 1, k:k + 1], wT[:, k, :], AX.X, ALU.max, apply_absolute_value=True))
                ve.wait_ge(S[skip], (3 * b + 2) if layer == 0 else b + 1)
                for k in range(kt):
                    link(V.tensor_reduce(col[:, 0, k:k + 1], acc[k][:, :], AX.X, ALU.max, apply_absolute_value=True))
                link(V.tensor_scalar(col[:, 0:2, 0:kt], col[:, 0:2, 0:kt], EPS_Q, None, ALU.max))
                link(V.reciprocal(col[:, 2, 0:kt], col[:, 1, 0:kt]))
                V.tensor_tensor(col[:, 3, 0:kt], col[:, 0, 0:kt], col[:, 2, 0:kt], ALU.mult).then_inc(S["s_arg"], 1)
                ve.wait_ge(S["s_pow"], r + 1)
                link(V.tensor_scalar(col[:, 5, 0:kt], col[:, 4, 0:kt], EPS_Q, None, ALU.max))
                link(V.reciprocal(col[:, 6, 0:kt], col[:, 5, 0:kt]))
                for k in range(kt):
                    link(V.tensor_scalar(dg[:, k, :], ident[:], col[:, 5, k:k + 1], None, ALU.mult))
                for k in range(kt):
                    ins = V.tensor_scalar(dg[:, 4 + k, :], ident[:], col[:, 6, k:k + 1], None, ALU.mult)
                    if k < kt - 1:
                        link(ins)
                ins.then_inc(S["diag_ready"], 1)
                ve.wait_ge(S["sbc_ps"], r + 1)
                for src, row, r0 in ((src_w, bank[4], TT), (src_x, bank[5], 0)):
                    for t in range(TT):
                        link(V.tensor_tensor(src[:, t, :], src[:, t, :], row[:, 0:width], ALU.mult))
                    for t in range(TT):
                        link(V.tensor_reduce(rr[:, 0, r0 + t:r0 + t + 1], src[:, t, :], AX.X, ALU.max,
                                             apply_absolute_value=True))
                link(V.tensor_scalar(rr[:, 1, :], rr[:, 0, :], EPS_Q, 1.0 / QMAX, ALU.max, ALU.mult))
                V.reciprocal(rr[:, 2, :], rr[:, 1, :]).then_inc(S["rinv_ready"], 1)
                for t in range(TT):
                    ins = V.tensor_scalar(dg[:, t, :], ident[:], rr[:, 1, TT + t:TT + t + 1], None, ALU.mult)
                    if t < TT - 1:
                        link(ins)
                ins.then_inc(S["wdiag_ready"], 1)
                for i in range(2 * TT):
                    ve.wait_ge(S["mg_ready"], 2 * TT * r + i + 1)
                    src = (src_x if i < TT else src_w)[:, i % TT, :]
                    V.tensor_scalar(q_rows[i // TT][:, (i % TT) * width:(i % TT + 1) * width], src, MAGIC, QMAX,
                                    ALU.subtract, ALU.min).then_inc(S["q_ready"], 1)
                for i in range(2):
                    ve.wait_ge(S["qT_ps"], 2 * r + i + 1)
                    for k in range(0, kt, 2):
                        ins = V.tensor_scalar(q_cols[i][:, k * T:(k + 2) * T], bankb[2 * i + k // 2][:, :], -QMAX, None,
                                              ALU.max)
                        if k < kt - 2:
                            link(ins)
                    ins.then_inc(S["qT_ready"], 1)
                assert link.n == LINKS[f"X{layer}"], (f"X{layer}", link.n)

            def batch_tail(b):
                ve.wait_ge(S["o_used"], NBLK * (b + 1))
                ve.wait_ge(S["x_res"], 16 * (b + 1))
                wait(ve, "out_done", 16 * b)
                for t in range(TT):
                    V.tensor_tensor(x2[:, t, :], xn[:, t, :], acc[t][:, :], ALU.add).then_inc(S["linkO"], 1)
                ve.wait_ge(S["linkO"], TT * 4 * b + TT)
                norm(3 * b + 1, x2)
                quant(b, 0, xn, guw, guwT, D, "tr_done")
                ve.wait_ge(S["wsc_ready"], 2 * b + 1)
                for t in range(TT):
                    ve.wait_ge(S["lin_ps"], TT * 2 * b + t + 1)
                    V.scalar_tensor_tensor(out=xn[:, t, :], in0=bank[4 + t][:, :], scalar=rr[:, 1, t:t + 1], in1=wsc,
                                           op0=ALU.mult, op1=ALU.mult).then_inc(S["h_ready"], 1)
                for t in range(TT):
                    ve.wait_ge(S["hth_ready"], TT * b + t + 1)
                    V.scalar_tensor_tensor(out=act[:, t, :], in0=hth[:, t, :], scalar=1.0, in1=xn[:, t, 0:INT],
                                           op0=ALU.add, op1=ALU.mult).then_inc(S["linkO"], 1)
                    ve.wait_ge(S["linkO"], TT * 4 * b + TT + t + 1)
                    V.scalar_tensor_tensor(out=act[:, t, :], in0=act[:, t, :], scalar=0.5, in1=xn[:, t, INT:D],
                                           op0=ALU.mult, op1=ALU.mult).then_inc(S["a_ready"], 1)
                quant(b, 1, act, dnw, dnwT, INT, "xc_ps")
                ve.wait_ge(S["wsc_ready"], 2 * b + 2)
                for t in range(TT):
                    ve.wait_ge(S["lin_ps"], TT * 2 * b + TT + t + 1)
                    V.scalar_tensor_tensor(out=xn[:, t, :], in0=bank[4 + t][:, :], scalar=rr[:, 1, t:t + 1], in1=wsc,
                                           op0=ALU.mult, op1=ALU.mult).then_inc(S["linkO"], 1)
                    ve.wait_ge(S["linkO"], TT * 4 * b + 2 * TT + t + 1)
                for t in range(TT):
                    V.tensor_tensor(x2[:, t, :], x2[:, t, :], xn[:, t, :], ALU.add).then_inc(S["linkO"], 1)
                ve.wait_ge(S["linkO"], TT * 4 * b + 4 * TT)
                norm(3 * b + 2, x2)

                link = Chain(ve, "linkG", LINKS["G"] * b)
                ve.wait_ge(S["lg_ps"], b + 1)
                link(V.tensor_copy(lg, bank[4][:, 0:TT * (NE + 1)].rearrange("p (t e) -> p t e", t=TT)))
                link(V.tensor_reduce(gm[:, 0, :], lg[:, :, 0:NE], AX.X, ALU.max))

                def rows(ap):
                    return ap.rearrange("p (t o) -> p t o", o=1).broadcast_to([P, TT, NE])

                V.tensor_tensor(pr[:, 0, :, :], lg[:, :, 0:NE], rows(gm[:, 0, :]), ALU.subtract
                                ).then_inc(S["ex_arg"], 1)
                ve.wait_ge(S["ex_ready"], b + 1)
                link(V.tensor_reduce(gm[:, 1, :], pr[:, 0, :, :], AX.X, ALU.add))
                link(V.reciprocal(gm[:, 2, :], gm[:, 1, :]))
                link.mark(V.tensor_tensor(pr[:, 0, :, :], pr[:, 0, :, :], rows(gm[:, 2, :]), ALU.mult))
                link.wait()
                carrier()
                for t in range(TT):
                    link.mark(V.max(top[:, t, :], pr[:, 0, t, :]))
                link.wait()
                carrier()
                for t in range(TT):
                    link.mark(V.max_index(topi[:, t, :], top[:, t, :], pr[:, 0, t, :]))
                link.wait()
                link(V.tensor_copy(topf[:, 0, :, :], topi[:, :, 0:2]))
                link(V.tensor_tensor(gm[:, 4, :], top[:, :, 0], top[:, :, 1], ALU.add))
                link(V.reciprocal(gm[:, 5, :], gm[:, 4, :]))
                link(V.scalar_tensor_tensor(out=topf[:, 1, :, :], in0=top[:, :, 0:2], scalar=0.5,
                                            in1=gm[:, 5, :].rearrange("p (t o) -> p t o", o=1).broadcast_to([P, TT, 2]),
                                            op0=ALU.mult, op1=ALU.mult))
                for i in range(2):
                    link(V.tensor_tensor(pr[:, 1 + i, :, :],
                                         iota[:, :].rearrange("p (o e) -> p o e", o=1).broadcast_to([P, TT, NE]),
                                         rows(topf[:, 0, :, i]), ALU.is_equal))
                    link(V.tensor_tensor(pr[:, 1 + i, :, :], pr[:, 1 + i, :, :], rows(topf[:, 1, :, i]), ALU.mult))
                link(V.tensor_tensor(comb[:, :, 0:NE], pr[:, 1, :, :], pr[:, 2, :, :], ALU.add))
                link(V.tensor_scalar(gm[:, 3, :], gm[:, 3, :], 1.0, None, ALU.add))
                link(V.reciprocal(gm[:, 3, :], gm[:, 3, :]))
                V.tensor_scalar(comb[:, :, NE], gm[:, 3, :], 0.5, None, ALU.mult).then_inc(S["comb_ready"], 1)
                assert link.n == LINKS["G"], ("G", link.n)

            stage_a(0)
            with ve.Fori(0, QUARTERS) as jj:
                step(0, jj, True, False)
            batch_tail(0)
            with ve.Fori(1, B) as b:
                stage_a(b)
                with ve.Fori(0, QUARTERS) as jj:
                    step(b, jj, True, True)
                finish(b - 1)
                batch_tail(b)
            with ve.Fori(0, QUARTERS) as jj:
                step(B, jj, False, True)
            finish(B - 1)

        @block.tensor
        def _(pe):
            mm = nc.tensor.matmul
            pe.wait_ge(S["const_in"], 16 * 7)
            pe.wait_ge(S["const_done"], 2)

            def norm_transposes(l):
                for t in range(TT):
                    pe.wait_ge(S["xn_ready"], TT * l + t + 1)
                    for k in range(KD):
                        ins = nc.tensor.transpose(acc[k][:, t * P:(t + 1) * P], xn[:, t, k * P:(k + 1) * P], ident[:])
                ins.then_inc(S["tr_done"], 1)

            def stage_a(b):
                norm_transposes(3 * b)
                pe.wait_ge(S["xT_ready"], KD * (b + 1))
                used = 0
                freed = []
                seen_z = 0
                for kind, m in ITEMS:
                    freed.append({"xi": ("xpad_ready", NBLK * b + m + 1), "z": ("z_ready", NBLK * b + m + 1),
                                  "bc": ("bc_ready", b + 1), "dt": ("dt_ready", b + 1),
                                  "dl": ("relu_ready", NBLK * b + m + 1)}[kind])
                for n, (kind, m) in enumerate(ITEMS):
                    ps = bank[4 + n % 4]
                    if n >= 4:
                        pe.wait_ge(S[freed[n - 4][0]], freed[n - 4][1])
                    else:
                        wait(pe, "cT_ready", b)
                    if kind in ("xi", "z"):
                        pe.wait_ge(w_in_s[used % W_RING], 16 * (W_USES // W_RING * b + used // W_RING + 1))
                        for k in range(KD):
                            ins = mm(ps[:, :], wst[:, used % W_RING, k * P:(k + 1) * P], xT[:, k, :],
                                     start=(k == 0), stop=(k == KD - 1))
                        ins.then_inc(S["a_ps"], 1)
                        used += 1
                        continue
                    if kind == "bc":
                        pe.wait_ge(S["u_ready"], NBLK * (b + 1))
                        for k in range(NBLK):
                            ins = mm(ps[0:2 * NS, :], xpw[:, k, DTR:DTR + 2 * NS], u[:, k, :],
                                     start=(k == 0), stop=(k == NBLK - 1))
                    elif kind == "dt":
                        for k in range(NBLK):
                            ins = mm(ps[:, :], xpw[:, k, 0:DTR], u[:, k, :], start=(k == 0), stop=(k == NBLK - 1))
                    else:
                        pe.wait_ge(S["dt_ready"], b + 1)
                        ins = mm(ps[:, :], dtw[:, m * P:(m + 1) * P], dtT, start=True, stop=True)
                    ins.then_inc(S["a_ps"], 1)
                pe.wait_ge(S["z_ready"], NBLK * (b + 1))

            def step(b, jj, scan, experts):
                q = 4 * b + jj
                qe = 4 * (b - 1) + jj

                def nsum(c):
                    jl, s = c // CHUNKS, c % 2
                    pe.wait_ge(S["hs_ready"], CH_Q * q + c + 1)
                    if c % CHUNKS == 0:
                        pe.wait_ge(S["y_done"], CREDIT + BLK_Q * q + jl - 1)
                    mm(Y[jl][:, :], ident[:], h[:, s, 0, :], start=(c % CHUNKS == 0),
                       stop=(c % CHUNKS == CHUNKS - 1)).then_inc(S["nsum_done"], 1)

                def phase(kind, i):
                    sl = SLOT[i]
                    if kind == "g":
                        pe.wait_ge(ew_in[sl], 32 * (SLOT_USES[sl] * qe + SLOT[:i + 1].count(sl)))
                        pe.wait_ge(S["t1_done"], ONE + EXP_Q * qe + i)
                    if kind == "u":
                        pe.wait_ge(S["t2_done"], ONE + EXP_Q * qe + i)
                    if kind in "gu":
                        o = 0 if kind == "g" else D
                        for k in range(KD):
                            ins = mm((G if kind == "g" else U)[:, :], ew[:, sl, o + k * P:o + (k + 1) * P], x3T[:, k, :],
                                     start=(k == 0), stop=(k == KD - 1))
                        ins.then_inc(S["g_done" if kind == "g" else "u_done"], 1)
                    else:
                        pe.wait_ge(S["hm_ready"], ONE + EXP_Q * qe + i + 1)
                        for t in range(TT):
                            ins = mm(acc[t][:, :], hm[:, i % 2, t * P:(t + 1) * P], ew[:, sl, 2 * D:3 * D],
                                     start=False, stop=False, skip_group_check=True)
                        ins.then_inc(S["down_done"], 1)

                for p in range(CH_Q):
                    if experts and p < len(PHASES):
                        phase(*PHASES[p])
                    if scan:
                        nsum(p)

            def experts_begin(b):
                pe.wait_ge(S["x3_ready"], KD * b)
                pe.wait_ge(S["cT_ready"], b)
                for t in range(TT):
                    mm(acc[t][:, :], zerob[:], zeros4,
                       start=True, stop=False, skip_group_check=True)

            def experts_end():
                for t in range(TT):
                    ins = mm(acc[t][:, :], zerob[:], zeros4, start=False, stop=True, skip_group_check=True)
                ins.then_inc(S["moe_done"], 1)

            zeros4 = zerob[:, 0:P].rearrange("p (o c) -> p o c", o=1).broadcast_to([P, 4, P])

            def linear(b, layer, width):
                r = 2 * b + layer
                kt = width // P
                pe.wait_ge(S["diag_ready"], r + 1)
                for dst, d0 in ((bank[4], 0), (bank[5], 4)):
                    for k in range(kt):
                        ins = mm(dst[:, k * P:(k + 1) * P], ones[:], dg[:, d0 + k, :], start=True, stop=True)
                ins.then_inc(S["sbc_ps"], 1)
                pe.wait_ge(S["wdiag_ready"], r + 1)
                for k in range(TT):
                    ins = mm(bank[6][:, k * P:(k + 1) * P], ones[:], dg[:, k, :], start=True, stop=True)
                ins.then_inc(S["wsc_ps"], 1)
                for i in range(2):
                    for t in range(TT):
                        pe.wait_ge(S["q_ready"], 2 * TT * r + TT * i + t + 1)
                        for k in range(kt):
                            o = (k % 2) * T + t * P
                            ins = nc.tensor.transpose(bankb[2 * i + k // 2][:, o:o + P],
                                                      q_rows[i][:, t * width + k * P:t * width + (k + 1) * P], identb[:])
                    ins.then_inc(S["qT_ps"], 1)
                pe.wait_ge(S["qT_ready"], 2 * r + 2)
                pe.wait_ge(S["wsc_ready"], r + 1)
                for t in range(TT):
                    for k in range(kt):
                        ins = mm(bank[4 + t][:, :], q_cols[0][:, k * T + t * P:k * T + (t + 1) * P],
                                 q_cols[1][:, k * T:(k + 1) * T], start=(k == 0), stop=(k == kt - 1))
                    ins.then_inc(S["lin_ps"], 1)

            def batch_tail(b):
                wait(pe, "fin_done", TT * b)
                pe.wait_ge(S["y_done"], CREDIT + NBLK * (b + 1))
                for k in range(NBLK):
                    n = len(W_ITEMS) + k
                    pe.wait_ge(w_in_s[n % W_RING], 16 * (W_USES // W_RING * b + n // W_RING + 1))
                    for t in range(TT):
                        ins = mm(acc[t][:, :], zg[:, k, t * P:(t + 1) * P], wst[:, n % W_RING, :],
                                 start=(k == 0), stop=(k == NBLK - 1))
                    ins.then_inc(S["o_used"], 1)
                norm_transposes(3 * b + 1)
                linear(b, 0, D)
                for t in range(TT):
                    pe.wait_ge(S["a_ready"], TT * b + t + 1)
                    for k in range(INT // P):
                        ins = nc.tensor.transpose(acc[k][:, t * P:(t + 1) * P], act[:, t, k * P:(k + 1) * P], ident[:])
                ins.then_inc(S["xc_ps"], 1)
                linear(b, 1, INT)
                norm_transposes(3 * b + 2)
                pe.wait_ge(S["x3_ready"], KD * (b + 1))
                for t in range(TT):
                    for k in range(KD):
                        ins = mm(bank[4][:, t * (NE + 1):(t + 1) * (NE + 1)], x3T[:, k, t * P:(t + 1) * P],
                                 gatew[:, k, :], start=(k == 0), stop=(k == KD - 1))
                ins.then_inc(S["lg_ps"], 1)
                pe.wait_ge(S["comb_ready"], b + 1)
                for t in range(TT):
                    ins = nc.tensor.transpose(bank[5][0:NE + 1, t * P:(t + 1) * P], comb[:, t, :], ident[:])
                ins.then_inc(S["comb_ps"], 1)

            stage_a(0)
            with pe.Fori(0, QUARTERS) as jj:
                step(0, jj, True, False)
            batch_tail(0)
            with pe.Fori(1, B) as b:
                stage_a(b)
                experts_begin(b)
                with pe.Fori(0, QUARTERS) as jj:
                    step(b, jj, True, True)
                experts_end()
                batch_tail(b)
            experts_begin(B)
            with pe.Fori(0, QUARTERS) as jj:
                step(B, jj, False, True)
            experts_end()


def kernel(**a):
    import concourse.bacc as bacc
    from concourse.bass_utils import run_bass_kernel_spmd as run

    a = {k: np.asarray(v) for k, v in a.items()}

    def blocks(w, rows):
        o, i = w.shape
        return np.ascontiguousarray(w.reshape(o // rows, rows, i // P, P).transpose(0, 3, 2, 1)).reshape(
            o // rows, P, (i // P) * rows)

    def cols(w):
        o, i = w.shape
        return np.ascontiguousarray(w.reshape(o, i // P, P).transpose(2, 1, 0))

    def tiles(v):
        return np.ascontiguousarray(v.reshape(v.shape[0] // P, P, -1).transpose(1, 0, 2))

    gu, dn = a["fside_BxS2xS2_0"], a["ctx_1024"]
    w1 = np.concatenate([a["L0_ffn_w1"], a["L0_ffn_ws_gate"].reshape(NSH, P, D)])
    w3 = np.concatenate([a["L0_ffn_w3"], a["L0_ffn_ws_up"].reshape(NSH, P, D)])
    w2 = np.concatenate([a["L0_ffn_w2"], a["L0_ffn_ws_down"].reshape(D, NSH, P).transpose(1, 0, 2)])
    up = [np.concatenate([blocks(w, P)[0] for w in ws])[None].reshape(NE + NSH, P, D) for ws in (w1, w3)]
    arrays = {
        "x": a["x"],
        "w_in": blocks(a["L0_attn_in_proj_weight"], P),
        "conv_w": tiles(a["L0_attn_conv1d_weight"].reshape(DI, TAPS)),
        "xp_w": cols(a["L0_attn_x_proj_weight"]),
        "dt_w": np.ascontiguousarray(a["L0_attn_dt_proj_weight"].T),
        "dt_b": tiles(a["L0_attn_dt_proj_bias"]).reshape(P, NBLK),
        "a_log": tiles(a["L0_attn_A_log"]),
        "d_skip": tiles(a["L0_attn_D"]).reshape(P, NBLK),
        "out_w": np.ascontiguousarray(a["L0_attn_out_proj_weight"].T).reshape(NBLK, P, D),
        "gu_w": np.stack([tiles(w) for w in gu]),
        "gu_wT": np.stack([cols(w) for w in gu]),
        "dn_w": np.stack([tiles(w) for w in dn]),
        "dn_wT": np.stack([cols(w) for w in dn]),
        "gate_w": cols(np.concatenate([a["L0_ffn_gate_w"], a["L0_ffn_shared_gate_w"]])),
        "exp_w": np.concatenate([up[0], up[1], np.ascontiguousarray(w2.transpose(0, 2, 1))], axis=2),
    }
    nc = bacc.Bacc("TRN2", target_bir_lowering=False, num_devices=1)
    args = {}
    for name, v in arrays.items():
        arrays[name] = np.ascontiguousarray(v)
        args[name] = nc.dram_tensor(f"in_{name}", v.shape, F32, kind="ExternalInput").ap()
    out = nc.dram_tensor("out_0", (B, T, D), F32, kind="ExternalOutput").ap()
    build(nc, out=out, **args)
    r = run(nc, [{f"in_{k}": v for k, v in arrays.items()}], core_ids=[0])
    return r.results[0]["out_0"]
```

```python
from contextlib import ExitStack

import numpy as np

import concourse.bass as bass
from concourse import mybir

F32 = mybir.dt.float32
BF16 = mybir.dt.bfloat16
U32 = mybir.dt.uint32
ALU = mybir.AluOpType
ACT = mybir.ActivationFunctionType
AX = mybir.AxisListType

P = 128
B = 4
T = 512
D = 512
DI = 1024
NS = 16
DTR = 128
TAPS = 4
INT = 256
NE = 16
NSH = 4
TT = T // P
KD = D // P
NBLK = DI // P
STEPS = 2
BLK_Q = NBLK // STEPS
EXP_Q = (NE + NSH) // STEPS
CN = 2
CHUNKS = NS // CN
CH_Q = BLK_Q * CHUNKS
W_RING = 4
SLOTS_E = 2
SHARED_Q = NSH // STEPS
EW = 2 * D + D
EPS_LN = 1e-5
EPS_Q = 1e-6
QMAX = 127.0
MAGIC = 1.5 * 2.0 ** 23
CREDIT = 4
ONE = 1
DOWN_CREDIT = SLOTS_E

ITEMS = ([("xi", m) for m in range(8)] + [("z", 0), ("z", 1), ("bc", 0), ("dt", 0), ("z", 2), ("z", 3)]
         + [("dl", j) for j in range(8)] + [("z", m) for m in range(4, 8)])
W_ITEMS = [it for it in ITEMS if it[0] in ("xi", "z")]
W_USES = len(W_ITEMS) + NBLK
PHASES = [("g", 0), ("u", 0)]
for _i in range(1, EXP_Q):
    PHASES += [("g", _i), ("u", _i), ("d", _i - 1)]
PHASES += [("d", EXP_Q - 1)]
SLOTS = [0, 1, 2, 4, 6, 8, 10, 12, 13, 15, 17, 18, 20, 21, 23]
TH_ORDER = [("xi", m) for m in range(8)] + [("z", m) for m in range(8)]
LINKS = {"A": 42, "LN": 8, "G": 24}
QUANT_LINKS = ((4 + 4 + 4, 17), (2 + 2 + 4, 17))



def build(nc, x, w_in, conv_w, xp_w, dt_w, dt_b, a_log, d_skip, out_w, gu_w, gu_wT, dn_w, dn_wT, gate_w,
          exp_w, out):
    with ExitStack() as ctx:
        def sb(name, shape, dt=F32):
            return ctx.enter_context(nc.sbuf_tensor(name, shape, dt))

        def sem(name):
            return ctx.enter_context(nc.semaphore(name))

        bc_dram = nc.dram_tensor("bc_dram", (2 * NS, T), F32, kind="Internal").ap()
        comb_dram = nc.dram_tensor("comb_dram", (NE + 1, T), F32, kind="Internal").ap()

        ident = sb("ident", [P, P])
        identb = sb("identb", [P, P], BF16)
        ones = sb("ones", [P, P])
        zerob = sb("zerob", [P, P], BF16)
        magic = sb("magic", [P, 1])
        halfpow = sb("halfpow", [P, 2, TT])
        iota = sb("iota", [P, NE])
        A_sb = sb("A_sb", [P, NBLK, NS])
        cw = sb("cw", [P, NBLK, TAPS])
        dtb = sb("dtb", [P, NBLK])
        dsk = sb("dsk", [P, NBLK])
        xpw = sb("xpw", [P, NBLK, DTR + 2 * NS])
        dtw = sb("dtw", [P, DI])
        gatew = sb("gatew", [P, KD, NE + 1])
        wst = sb("wst", [P, W_RING, 512])
        ew = sb("ew", [P, SLOTS_E, EW])
        comb_bc = sb("comb_bc", [P, SLOTS_E, T])
        x2 = sb("x2", [P, TT, D])
        x3T = sb("x3T", [P, KD, T])
        delta = sb("delta", [P, NBLK, T])
        u = sb("u", [P, NBLK, T])
        zg = sb("zg", [P, NBLK, T])
        BB = sb("BB", [P, NS, T])
        CB = sb("CB", [P, NS, T])
        du = sb("du", [P, 1, T])
        work = sb("work", [P, 6144])
        pairs = sb("pairs", [P, 4, T])
        etm = sb("etm", [P, 2, T])
        hm = sb("hm", [P, 2, T])
        st = sb("st", [P, TT, 6])
        mv = sb("mv", [P, TT, 2])
        rstd = sb("rstd", [P, TT])
        col = sb("col", [P, 8, 4])
        rr = sb("rr", [P, 3, 2 * TT])
        dtT = hm[:, 0, :]
        bcS = hm[0:2 * NS, 1, :]

        dA = work[:, 0:2048].rearrange("p (s n t) -> p s n t", s=2, n=CN)
        dBu = work[:, 2048:6144].rearrange("p (s n t) -> p s n t", s=4, n=CN)
        xpad = work[:, 0:1030].rearrange("p (s t) -> p s t", s=2)
        xT = work[:, 2048:4096].rearrange("p (k t) -> p k t", k=KD)
        xn = work[:, 4096:6144].rearrange("p (k t) -> p k t", k=TT)
        a_st = work[:, 1040:1064].rearrange("p (t i) -> p t i", t=TT)
        a_mv = work[:, 1064:1072].rearrange("p (t i) -> p t i", t=TT)
        a_rstd = work[:, 1072:1076]
        guwT = BB[:, 0:4, :]
        guw = CB[:, 0:4, :]
        zb = BB[:, 4:8, :].rearrange("p a b -> p (a b)").bitcast(BF16)
        q_rows = [zb[:, 0:2048], zb[:, 2048:4096]]
        zb = CB[:, 4:8, :].rearrange("p a b -> p (a b)").bitcast(BF16)
        q_cols = [zb[:, 0:2048], zb[:, 2048:4096]]
        x1n = BB[:, 8:12, :]
        dnw = CB[:, 8:10, :].rearrange("p a (b i) -> p (a b) i", b=2)
        dnwT = CB[:, 10:12, :]
        hth = BB[:, 12:14, :].rearrange("p a (b i) -> p (a b) i", b=2)
        act = BB[:, 14:16, :].rearrange("p a (b i) -> p (a b) i", b=2)
        dg = CB[:, 12:14, :].rearrange("p a (b c) -> p (a b) c", b=4)
        wsc = CB[:, 14, :]
        cT = CB[0:NE + 1, 15, :]
        rt = CB[:, 12, :]
        lg = rt[:, 0:68].rearrange("p (t e) -> p t e", t=TT)
        comb = rt[:, 68:136].rearrange("p (t e) -> p t e", t=TT)
        pr = rt[:, 136:328].rearrange("p (i t e) -> p i t e", i=3, t=TT)
        top = rt[:, 328:360].rearrange("p (t e) -> p t e", t=TT)
        topi = rt[:, 360:392].bitcast(U32).rearrange("p (t e) -> p t e", t=TT)
        topf = rt[:, 392:408].rearrange("p (i t e) -> p i t e", i=2, t=TT)
        gm = rt[:, 408:432].rearrange("p (i t) -> p i t", i=6)
        sp_e, sp_err, sp_ln, sp_inv = (
            [work[:, o + i * T:o + (i + 1) * T] for o in (4096, 0)] for i in range(4))
        bank = [ctx.enter_context(nc.psum_tensor(f"bank{i}", [P, 512], F32)) for i in range(8)]
        acc = bank[0:4]
        accb = [t[:, :].bitcast(BF16) for t in acc]
        G, U = bank[4], bank[5]
        Y = [bank[6], bank[7]]

        S = {n: sem(n) for n in (
            "const_in a_var_ready a_rstd_ready a_xn_ready a_tr_done zero_done ident_done const_done a_exp x_in x_res var_ready rstd_ready xn_ready tr_done xT_ready a_ps "
            "xpad_ready conv_done th_ready u_ready z_ready bc_ready bc_out dt_ready delta_ready "
            "du_ready dbu_ready da_ready scan_done prod_done hs_ready nsum_done y_done "
            "g_done u_done eth_ready t1_done t2_done hm_ready down_done moe_done fin_done out_done "
            "o_used xw_in xc_ps s_arg s_pow diag_ready sbc_ps rinv_ready wdiag_ready mg_ready wsc_ps "
            "wsc_ready q_ready qT_ps qT_ready lin_ps h_ready hth_ready a_ready x3_ready lg_ps ex_arg "
            "ex_ready comb_ready comb_ps cT_ready comb_out init linkA linkAN linkLN linkX linkG linkO linkS linkSP sp_e_ready relu_ready sp_inv_ready sp_err_ready sum_ready").split()}
        w_in_s = [sem(f"w_in{i}") for i in range(W_RING)]
        ew_up = [sem(f"ew_up{i}") for i in range(SLOTS_E)]
        ew_down = [sem(f"ew_down{i}") for i in range(SLOTS_E)]
        bcast = [sem(f"bcast{i}") for i in range(4)]

        def wait(eng, name, value):
            s = S[name] if isinstance(name, str) else name
            if not isinstance(value, int) or value > 0:
                eng.wait_ge(s, value)

        class Chain:

            def __init__(self, eng, name, base):
                self.eng, self.sem, self.base, self.n = eng, S[name], base, 0

            def mark(self, ins):
                self.n += 1
                ins.then_inc(self.sem, 1)

            def wait(self):
                self.eng.wait_ge(self.sem, self.base + self.n)

            def __call__(self, ins):
                self.mark(ins)
                self.wait()

        block = ctx.enter_context(nc.Block())

        @block.sync
        def _(sp):
            for dst, src in ((cw, conv_w), (dtb, dt_b), (dsk, d_skip), (A_sb, a_log), (xpw, xp_w),
                             (dtw, dt_w), (gatew, gate_w)):
                sp.dma_start(dst[:], src).then_inc(S["const_in"], 16)

            def batch_x(b):
                return x[bass.ds(b, 1), :, :].rearrange("o (t p) d -> p (o t) d", p=P)

            def weight(b, n, src):
                m = n - W_RING
                if m < 0:
                    wait(sp, "o_used", NBLK * b + m + 1)
                elif m < len(W_ITEMS):
                    sp.wait_ge(S["a_ps"], len(ITEMS) * b + ITEMS.index(W_ITEMS[m]) + 1)
                else:
                    sp.wait_ge(S["o_used"], NBLK * b + m - len(W_ITEMS) + 1)
                sp.dma_start(wst[:, n % W_RING, :], src).then_inc(w_in_s[n % W_RING], 16)

            def load_a(b):
                wait(sp, "hs_ready", 0 if isinstance(b, int) else CREDIT + STEPS * CH_Q * b)
                sp.dma_start(xn, batch_x(b)).then_inc(S["x_in"], 16)
                n = 0
                for kind, m in ITEMS:
                    if kind in ("xi", "z"):
                        weight(b, n, w_in[m + (NBLK if kind == "z" else 0)])
                        n += 1
                    if (kind, m) == ("z", 3):
                        sp.wait_ge(S["bc_ready"], 1 + b)
                        sp.dma_start(bc_dram, bcS).then_inc(S["bc_out"], 16)
                        sp.wait_ge(S["bc_out"], 16 * b + 16)
                        wait(sp, "q_ready", 4 * TT * (b - 1) + 2 * TT)
                        broadcast(b, 0)
                wait(sp, "lin_ps", 2 * TT * b)
                broadcast(b, 1)
                wait(sp, "tr_done", 2 * b)
                broadcast(b, 2)
                if not isinstance(b, int):
                    comb_rows(b - 1)
                    sp.wait_ge(S["comb_out"], 16 * b)
                broadcast(b, 3)

            def broadcast(b, g):
                for half, dst in enumerate((BB, CB)):
                    rows = bc_dram[half * NS + 4 * g:half * NS + 4 * g + 4, :]
                    sp.dma_start(dst[:, 4 * g:4 * g + 4, :],
                                 rows.rearrange("n t -> (n t)").partition_broadcast(P)
                                 .rearrange("p (n t) -> p n t", n=4)).then_inc(bcast[g], 16)

            def load_e(be, jj):
                qe = STEPS * be + jj
                sp.wait_ge(S["comb_out"], 16 * be + 16)
                for i in range(EXP_Q):
                    routed = EXP_Q - SHARED_Q
                    e = jj * routed + i if i < routed else NE + jj * SHARED_Q + (i - routed)
                    src = exp_w[bass.ds(e, 1), :, :].rearrange("o p n -> p (o n)")
                    sp.wait_ge(S["u_done"], EXP_Q * qe + i + 1)
                    sp.dma_start(ew[:, i % SLOTS_E, 0:2 * D], src[:, 0:2 * D]).then_inc(ew_up[i % SLOTS_E], 16)
                    sp.wait_ge(S["down_done"], EXP_Q * qe + i + 1)
                    sp.dma_start(ew[:, i % SLOTS_E, 2 * D:3 * D], src[:, 2 * D:3 * D]).then_inc(ew_down[i % SLOTS_E], 16)
                    src = comb_dram[bass.ds(e, 1), :] if i < routed else comb_dram[NE:NE + 1, :]
                    sp.dma_start(comb_bc[:, i % SLOTS_E, :], src.rearrange("o t -> (o t)").partition_broadcast(P)
                                 ).then_inc(ew_down[i % SLOTS_E], 16)

            def load_o(b):
                sp.wait_ge(S["prod_done"], STEPS * CH_Q * (b + 1))
                sp.dma_start(x1n, batch_x(b)).then_inc(S["x_res"], 16)
                for k in range(NBLK):
                    weight(b, len(W_ITEMS) + k, out_w[k])
                for dst, src in ((guw, gu_w), (guwT, gu_wT), (dnw, dn_w), (dnwT, dn_wT)):
                    sp.dma_start(dst, src[bass.ds(b, 1)].rearrange("o p k n -> p (o k) n")
                                 ).then_inc(S["xw_in"], 16)

            def store(be):
                sp.wait_ge(S["fin_done"], TT * be + TT)
                sp.dma_start(out[bass.ds(be, 1), :, :].rearrange("o (t p) d -> p (o t) d", p=P), x2[:]
                             ).then_inc(S["out_done"], 16)

            def comb_rows(b):
                sp.wait_ge(S["cT_ready"], b + 1)
                sp.dma_start(comb_dram, cT).then_inc(S["comb_out"], 16)

            load_a(0)
            load_o(0)
            with sp.Fori(1, B) as b:
                load_a(b)
                with sp.Fori(0, STEPS) as jj:
                    load_e(b - 1, jj)
                store(b - 1)
                load_o(b)
            comb_rows(B - 1)
            with sp.Fori(0, STEPS) as jj:
                load_e(B - 1, jj)
            store(B - 1)
            sp.wait_ge(S["out_done"], 16 * B)

        @block.gpsimd
        def _(pool):
            nc.gpsimd.memset(ident[:], 0.0).then_inc(S["zero_done"], 1)
            nc.gpsimd.memset(ones[:], 1.0)
            nc.gpsimd.memset(zerob[:], 0.0)
            nc.gpsimd.memset(magic[:], MAGIC)
            nc.gpsimd.memset(halfpow[:, 0, :], 0.5)
            nc.gpsimd.memset(halfpow[:, 1, :], -0.5).then_inc(S["ident_done"], 1)
            pool.wait_ge(S["zero_done"], 1)
            nc.gpsimd.affine_select(out=ident[:], in_=ident[:], compare_op=ALU.not_equal, fill=1.0, base=0,
                                    pattern=[[-1, P]], channel_multiplier=1).then_inc(S["ident_done"], 1)
            pool.wait_ge(S["ident_done"], 2)
            nc.gpsimd.tensor_copy(identb[:], ident[:]).then_inc(S["const_done"], 1)
            nc.gpsimd.iota(iota[:], pattern=[[1, NE]], base=0, channel_multiplier=0,
                           allow_small_or_imprecise_dtypes=True).then_inc(S["const_done"], 1)

            def power(ready, value, dst, src, exponent, done):
                pool.wait_ge(S[ready], value)
                nc.gpsimd.tensor_tensor(dst, src, exponent, ALU.pow).then_inc(S[done], 1)

            def norm(l):
                power("var_ready", l + 1, rstd[:], mv[:, :, 1], halfpow[:, 1, :], "rstd_ready")

            def mlp_step(b, k):
                if k == 0:
                    norm(2 * b)
                elif k in (2, 7):
                    kt = (KD, 2)[k // 7]
                    power("s_arg", 2 * b + k // 7 + 1, col[:, 4, 0:kt], col[:, 3, 0:kt], halfpow[:, 0, 0:kt], "s_pow")
                elif k == 11:
                    norm(2 * b + 1)

            def stage_a(b, mlp):
                power("a_var_ready", b + 1, a_rstd, a_mv[:, :, 1], halfpow[:, 1, :], "a_rstd_ready")
                for n, (kind, m) in enumerate(ITEMS):
                    if kind == "dl":
                        softplus(b, m)
                    if mlp and n in SLOTS:
                        mlp_step(b - 1, SLOTS.index(n))

            def step(b, jj, scan, experts):
                q = STEPS * b + jj
                qe = STEPS * (b - 1) + jj
                if scan:
                    pool.wait_ge(S["delta_ready"], NBLK * (b + 1))
                    pool.wait_ge(S["u_ready"], NBLK * (b + 1))
                    pool.wait_ge(S["a_ps"], len(ITEMS) * (b + 1))

                def chunk(c):
                    jl, s, n0 = c // CHUNKS, c % 4, CN * (c % CHUNKS)
                    if c % CHUNKS == 0:
                        dj = delta[:, bass.ds(jj * BLK_Q + jl, 1), :].rearrange("p o t -> p (o t)")
                        uj = u[:, bass.ds(jj * BLK_Q + jl, 1), :].rearrange("p o t -> p (o t)")
                        pool.wait_ge(S["dbu_ready"], ONE + CH_Q * q + c)
                        nc.gpsimd.tensor_tensor(du[:, 0, :], dj, uj, ALU.mult).then_inc(S["du_ready"], 1)
                        pool.wait_ge(S["du_ready"], BLK_Q * q + jl + 1)
                    pool.wait_ge(bcast[n0 // 4], 32 * (b + 1))
                    pool.wait_ge(S["hs_ready"], CREDIT + CH_Q * q + c - 3)
                    nc.gpsimd.tensor_tensor(
                        dBu[:, s, :, :], du[:, 0:1, :].broadcast_to([P, CN, T]),
                        BB[:, n0:n0 + CN, :], ALU.mult).then_inc(S["dbu_ready"], 1)

                def gate(i):
                    pool.wait_ge(S["t2_done"], ONE + EXP_Q * qe + i + 1)
                    pool.wait_ge(S["down_done"], EXP_Q * qe + i + 1)
                    pool.wait_ge(ew_down[i % SLOTS_E], 32 * (EXP_Q // SLOTS_E * qe + i // SLOTS_E + 1))
                    nc.gpsimd.tensor_tensor(hm[:, i % 2, :], etm[:, 1, :], comb_bc[:, i % SLOTS_E, :],
                                            ALU.mult).then_inc(S["hm_ready"], 1)

                for p in range(CH_Q):
                    if scan:
                        chunk(p)
                    if experts and p - 2 >= 0 and ("u", p - 2) and p - 2 < len(PHASES) and PHASES[p - 2][0] == "u":
                        gate(PHASES[p - 2][1])

            def softplus(b, m):
                pool.wait_ge(S["sp_inv_ready"], NBLK * b + m + 1)
                nc.gpsimd.tensor_tensor(delta[:, m, :], delta[:, m, :], sp_ln[m % 2], ALU.add
                                        ).then_inc(S["sum_ready"], 1)
                pool.wait_ge(S["sum_ready"], NBLK * b + m + 1)
                pool.wait_ge(S["sp_err_ready"], NBLK * b + m + 1)
                nc.gpsimd.tensor_tensor(delta[:, m, :], delta[:, m, :], sp_err[m % 2], ALU.subtract
                                        ).then_inc(S["delta_ready"], 1)

            stage_a(0, False)
            with pool.Fori(0, STEPS) as jj:
                step(0, jj, True, False)
            with pool.Fori(1, B) as b:
                stage_a(b, True)
                with pool.Fori(0, STEPS) as jj:
                    step(b, jj, True, True)
            for k in range(len(SLOTS)):
                mlp_step(B - 1, k)
            with pool.Fori(0, STEPS) as jj:
                step(B, jj, False, True)

        @block.scalar
        def _(sc):
            sc.wait_ge(S["const_in"], 16 * 7)
            nc.scalar.activation(A_sb[:], A_sb[:], ACT.Exp).then_inc(S["a_exp"], 1)

            def stage_a(b, mlp):
                sc.wait_ge(S["a_tr_done"], b + 1)
                for k in range(2):
                    nc.scalar.copy(xT[:, k, :], bank[4 + k][:, :]).then_inc(S["xT_ready"], 1)

                def tanh_x(m):
                    r = m
                    sc.wait_ge(S["conv_done"], NBLK * b + m + 1)
                    if r >= 2:
                        sc.wait_ge(S["u_ready"], NBLK * b + r - 1)
                    nc.scalar.activation(etm[:, r % 2, :], u[:, m, :], ACT.Tanh).then_inc(S["th_ready"], 1)

                for n, (kind, m) in enumerate(ITEMS):
                    sc.wait_ge(S["a_ps"], len(ITEMS) * b + n + 1)
                    ps = bank[4 + n % 4]
                    if kind == "xi":
                        if m >= 2:
                            sc.wait_ge(S["conv_done"], NBLK * b + m - 1)
                        nc.scalar.copy(xpad[:, m % 2, TAPS - 1:TAPS - 1 + T], ps[:, :]).then_inc(S["xpad_ready"], 1)
                        if m >= 1:
                            tanh_x(m - 1)
                    elif kind == "z":
                        if m == 0:
                            tanh_x(NBLK - 1)
                            sc.wait_ge(S["u_ready"], NBLK * b + NBLK - 1)
                        elif m == 1:
                            sc.wait_ge(S["u_ready"], NBLK * b + NBLK)
                        else:
                            sc.wait_ge(S["z_ready"], NBLK * b + m - 1)
                        nc.scalar.activation(etm[:, m % 2, :], ps[:, :], ACT.Tanh, scale=0.5
                                             ).then_inc(S["th_ready"], 1)
                    elif kind == "bc":
                        nc.scalar.copy(bcS, ps[0:2 * NS, :]).then_inc(S["bc_ready"], 1)
                    elif kind == "dt":
                        nc.scalar.copy(dtT, ps[:, :]).then_inc(S["dt_ready"], 1)
                    else:
                        s = m % 2
                        if m < 2:
                            sc.wait_ge(S["conv_done"], NBLK * (b + 1))
                        else:
                            sc.wait_ge(S["delta_ready"], NBLK * b + m - 1)
                        nc.scalar.activation(sp_e[s], ps[:, :], ACT.Abs, bias=dtb[:, m:m + 1]
                                             ).then_inc(S["linkSP"], 1)
                        sc.wait_ge(S["linkSP"], 2 * (NBLK * b + m) + 1)
                        nc.scalar.activation(sp_e[s], sp_e[s], ACT.Exp, scale=-1.0).then_inc(S["sp_e_ready"], 1)
                        sc.wait_ge(S["sp_e_ready"], NBLK * b + m + 1)
                        nc.scalar.activation(sp_ln[s], sp_e[s], ACT.Ln, bias=ones[:, 0:1]).then_inc(S["linkSP"], 1)
                        nc.scalar.activation(delta[:, m, :], ps[:, :], ACT.Relu, bias=dtb[:, m:m + 1]
                                             ).then_inc(S["relu_ready"], 1)
                        sc.wait_ge(S["linkSP"], 2 * (NBLK * b + m) + 2)
                        nc.scalar.activation(sp_inv[s], sp_ln[s], ACT.Exp, scale=-1.0
                                             ).then_inc(S["sp_inv_ready"], 1)
                    if mlp and n in SLOTS:
                        mlp_step(b - 1, SLOTS.index(n))

            def step(b, jj, scan, experts):
                q = STEPS * b + jj
                qe = STEPS * (b - 1) + jj
                if scan:
                    sc.wait_ge(S["delta_ready"], NBLK * (b + 1))

                def chunk(c):
                    jl, s, n0 = c // CHUNKS, c % 2, CN * (c % CHUNKS)
                    dj = delta[:, bass.ds(jj * BLK_Q + jl, 1), 1:T].rearrange("p o t -> p (o t)")
                    sc.wait_ge(S["scan_done"], 2 + CH_Q * q + c - 1)
                    for i in range(CN):
                        a = A_sb[:, bass.ds(jj * BLK_Q + jl, 1), n0 + i:n0 + i + 1].rearrange("p o n -> p (o n)")
                        ins = nc.scalar.activation(dA[:, s, i, 1:T], dj, ACT.Exp, scale=a)
                    ins.then_inc(S["da_ready"], 1)

                def tanh_g(i):
                    sc.wait_ge(S["g_done"], EXP_Q * qe + i + 1)
                    sc.wait_ge(S["t1_done"], ONE + EXP_Q * qe + i)
                    nc.scalar.activation(etm[:, 0, :], G[:, :], ACT.Tanh, scale=0.5).then_inc(S["eth_ready"], 1)

                for p in range(CH_Q):
                    if scan:
                        chunk(p)
                    if experts and p >= 1 and p - 1 < len(PHASES) and PHASES[p - 1][0] == "g":
                        tanh_g(PHASES[p - 1][1])

            def magic_rows(b, layer, src_x, src_w):
                sc.wait_ge(S["rinv_ready"], 2 * b + layer + 1)
                for i in range(2 * TT):
                    src = (src_x if i < TT else src_w)[:, i % TT, :]
                    nc.scalar.activation(src, src, ACT.Identity, scale=rr[:, 2, i:i + 1], bias=magic[:, 0:1]
                                         ).then_inc(S["mg_ready"], 1)

            def weight_scales(b, layer):
                sc.wait_ge(S["wsc_ps"], 2 * b + layer + 1)
                nc.scalar.copy(wsc, acc[2][:, :]).then_inc(S["wsc_ready"], 1)

            def mlp_step(b, k):
                if k == 3:
                    magic_rows(b, 0, x1n, guw)
                elif k == 4:
                    weight_scales(b, 0)
                elif k == 6:
                    for t in range(TT):
                        sc.wait_ge(S["h_ready"], TT * b + t + 1)
                        nc.scalar.activation(hth[:, t, :], x1n[:, t, 0:INT], ACT.Tanh, scale=0.5
                                             ).then_inc(S["hth_ready"], 1)
                elif k == 8:
                    magic_rows(b, 1, act, dnw)
                elif k == 9:
                    weight_scales(b, 1)
                elif k == 13:
                    sc.wait_ge(S["tr_done"], 2 * b + 2)
                    for i in range(KD):
                        nc.scalar.copy(x3T[:, i, :], acc[i][:, :]).then_inc(S["x3_ready"], 1)
                elif k == 14:
                    sc.wait_ge(S["ex_arg"], b + 1)
                    nc.scalar.activation(pr[:, 0, :, :], pr[:, 0, :, :], ACT.Exp)
                    nc.scalar.activation(gm[:, 3, :], lg[:, :, NE], ACT.Exp, scale=-1.0).then_inc(S["ex_ready"], 1)

            def combine_rows(b):
                sc.wait_ge(S["comb_ps"], b + 1)
                nc.scalar.copy(cT, acc[1][0:NE + 1, :]).then_inc(S["cT_ready"], 1)

            stage_a(0, False)
            with sc.Fori(0, STEPS) as jj:
                step(0, jj, True, False)
            with sc.Fori(1, B) as b:
                stage_a(b, True)
                combine_rows(b - 1)
                with sc.Fori(0, STEPS) as jj:
                    step(b, jj, True, True)
            for k in range(len(SLOTS)):
                mlp_step(B - 1, k)
            combine_rows(B - 1)
            with sc.Fori(0, STEPS) as jj:
                step(B, jj, False, True)

        @block.vector
        def _(ve):
            V = nc.vector
            for i, (free, n) in enumerate((("scan_done", 2), ("y_done", 2), ("hs_ready", CREDIT), ("nsum_done", CREDIT),
                                           ("t1_done", ONE), ("t2_done", ONE), ("hm_ready", ONE),
                                           ("dbu_ready", ONE), ("u_done", DOWN_CREDIT), ("down_done", DOWN_CREDIT))):
                V.memset(comb_bc[:, 0, i:i + 1], 0.0).then_inc(S[free], n)
            ve.wait_ge(S["const_in"], 16 * 7)
            V.tensor_scalar(cw[:], cw[:], 0.5, None, ALU.mult).then_inc(S["init"], 1)
            ve.wait_ge(S["a_exp"], 1)
            V.tensor_scalar(A_sb[:], A_sb[:], -1.0, None, ALU.mult).then_inc(S["init"], 1)
            ve.wait_ge(S["init"], 2)
            ve.wait_ge(S["const_done"], 2)

            def carrier():
                V.memset(rr[:, 0, 0:1], 0.0)

            def norm_stats(l, src, st, mv, var_ready, link):
                for t in range(TT):
                    link.mark(V.bn_stats(st[:, t, :], src[:, t, :]))
                link.wait()
                carrier()
                for t in range(TT):
                    link.mark(V.bn_aggr(mv[:, t, :], st[:, t, :]))
                link.wait()
                V.tensor_scalar(mv[:, :, 1], mv[:, :, 1], EPS_LN, None, ALU.add).then_inc(S[var_ready], 1)
                assert link.n == LINKS["LN"], ("LN", link.n)

            def norm_apply(l, src, dst, mv, rstd, var_ready, rstd_ready, xn_ready):
                ve.wait_ge(S[rstd_ready], l + 1)
                ve.wait_ge(S[var_ready], l + 1)
                for t in range(TT):
                    V.tensor_scalar(dst[:, t, :], src[:, t, :], mv[:, t, 0:1], rstd[:, t:t + 1],
                                    ALU.subtract, ALU.mult).then_inc(S[xn_ready], 1)

            def stage_a(b, mlp):
                link = Chain(ve, "linkA", LINKS["A"] * b)
                ve.wait_ge(S["x_in"], 16 * (b + 1))
                norm_stats(b, xn, a_st, a_mv, "a_var_ready", Chain(ve, "linkAN", LINKS["LN"] * b))
                norm_apply(b, xn, xn, a_mv, a_rstd, "a_var_ready", "a_rstd_ready", "a_xn_ready")
                link(V.memset(xpad[:, :, 0:TAPS - 1], 0.0))
                ve.wait_ge(S["a_tr_done"], b + 1)
                for k in range(2, KD):
                    V.tensor_copy(xT[:, k, :], bank[4 + k][:, :]).then_inc(S["xT_ready"], 1)

                def conv(m):
                    xp = xpad[:, m % 2, :]
                    ve.wait_ge(S["xpad_ready"], NBLK * b + m + 1)
                    link(V.tensor_scalar(u[:, m, :], xp[:, 0:T], cw[:, m, 0:1], None, ALU.mult))
                    for j in range(1, TAPS):
                        ins = V.scalar_tensor_tensor(out=u[:, m, :], in0=xp[:, j:j + T], scalar=cw[:, m, j:j + 1],
                                                     in1=u[:, m, :], op0=ALU.mult, op1=ALU.add)
                        if j < TAPS - 1:
                            link(ins)
                    ins.then_inc(S["conv_done"], 1)

                def silu_x(m):
                    ve.wait_ge(S["th_ready"], 2 * NBLK * b + m + 1)
                    V.scalar_tensor_tensor(out=u[:, m, :], in0=etm[:, m % 2, :], scalar=1.0, in1=u[:, m, :],
                                           op0=ALU.add, op1=ALU.mult).then_inc(S["u_ready"], 1)

                def silu_z(m, n):
                    ve.wait_ge(S["th_ready"], 2 * NBLK * b + NBLK + m + 1)
                    V.scalar_tensor_tensor(out=zg[:, m, :], in0=etm[:, m % 2, :], scalar=1.0,
                                           in1=bank[4 + n % 4][:, :], op0=ALU.add, op1=ALU.mult
                                           ).then_inc(S["z_ready"], 1)

                def softplus(m):
                    s = m % 2
                    ve.wait_ge(S["sp_e_ready"], NBLK * b + m + 1)
                    link(V.tensor_scalar(sp_err[s], sp_e[s], 1.0, -1.0, ALU.add, ALU.add))
                    link(V.tensor_tensor(sp_err[s], sp_err[s], sp_e[s], ALU.subtract))
                    ve.wait_ge(S["sp_inv_ready"], NBLK * b + m + 1)
                    V.tensor_tensor(sp_err[s], sp_err[s], sp_inv[s], ALU.mult).then_inc(S["sp_err_ready"], 1)

                for n, (kind, m) in enumerate(ITEMS):
                    if kind == "xi":
                        conv(m)
                        if m >= 1:
                            silu_x(m - 1)
                    elif kind == "z":
                        if m == 0:
                            silu_x(NBLK - 1)
                        silu_z(m, n)
                    elif kind == "dl":
                        softplus(m)
                    if mlp and n in SLOTS:
                        mlp_step(b - 1, SLOTS.index(n))
                ve.wait_ge(S["delta_ready"], NBLK * (b + 1))
                link.mark(V.memset(dA[:, :, :, 0:1], 0.0))
                assert link.n == LINKS["A"], ("A", link.n)

            def step(b, jj, scan, experts):
                q = STEPS * b + jj
                qe = STEPS * (b - 1) + jj

                if scan:
                    ve.wait_ge(S["linkA"], LINKS["A"] * (b + 1))

                def scan_chunk(c):
                    s = c % 4
                    ve.wait_ge(S["da_ready"], CH_Q * q + c + 1)
                    ve.wait_ge(S["dbu_ready"], ONE + CH_Q * q + c + 1)
                    state = dBu[:, s, :, :].rearrange("p n t -> p (n t)")
                    V.tensor_tensor_scan(state, dA[:, c % 2, :, :].rearrange("p n t -> p (n t)"), state,
                                         0.0, ALU.mult, ALU.add).then_inc(S["scan_done"], 1)

                def product(c):
                    s, n0 = c % 4, CN * (c % CHUNKS)
                    ve.wait_ge(S["scan_done"], 2 + CH_Q * q + c + 1)
                    ve.wait_ge(bcast[n0 // 4], 32 * (b + 1))
                    V.tensor_tensor(dBu[:, s, :, :], dBu[:, s, :, :], CB[:, n0:n0 + CN, :], ALU.mult
                                    ).then_inc(S["prod_done"], 1)

                def pair_sum(c):
                    s = c % 4
                    ve.wait_ge(S["prod_done"], CH_Q * q + c + 1)
                    ve.wait_ge(S["nsum_done"], CREDIT + CH_Q * q + c - 3)
                    V.tensor_tensor(pairs[:, s, :], dBu[:, s, 0, :], dBu[:, s, 1, :], ALU.add
                                    ).then_inc(S["hs_ready"], 1)

                def gated(jl):
                    ujl = u[:, bass.ds(jj * BLK_Q + jl, 1), :].rearrange("p o t -> p (o t)")
                    zjl = zg[:, bass.ds(jj * BLK_Q + jl, 1), :].rearrange("p o t -> p (o t)")
                    djl = dsk[:, bass.ds(jj * BLK_Q + jl, 1)]
                    ve.wait_ge(S["nsum_done"], CREDIT + CH_Q * q + CHUNKS * (jl + 1))
                    V.scalar_tensor_tensor(out=ujl, in0=ujl, scalar=djl, in1=Y[jl % 2][:, :], op0=ALU.mult,
                                           op1=ALU.add).then_inc(S["linkS"], 1)
                    ve.wait_ge(S["linkS"], BLK_Q * q + jl + 1)
                    V.scalar_tensor_tensor(out=zjl, in0=ujl, scalar=0.5, in1=zjl, op0=ALU.mult, op1=ALU.mult
                                           ).then_inc(S["y_done"], 1)

                def expert_gate(i):
                    ve.wait_ge(S["eth_ready"], EXP_Q * qe + i + 1)
                    ve.wait_ge(S["hm_ready"], ONE + EXP_Q * qe + i)
                    V.scalar_tensor_tensor(out=etm[:, 1, :], in0=etm[:, 0, :], scalar=1.0, in1=G[:, :],
                                           op0=ALU.add, op1=ALU.mult).then_inc(S["t1_done"], 1)

                def expert_up(i):
                    ve.wait_ge(S["u_done"], DOWN_CREDIT + EXP_Q * qe + i + 1)
                    ve.wait_ge(S["t1_done"], ONE + EXP_Q * qe + i + 1)
                    V.tensor_tensor(etm[:, 1, :], etm[:, 1, :], U[:, :], ALU.mult).then_inc(S["t2_done"], 1)

                for p in range(CH_Q + 1):
                    if scan:
                        if p < CH_Q:
                            scan_chunk(p)
                        if p >= 1:
                            pair_sum(p - 1)
                        if p < CH_Q:
                            product(p)
                        if p == CH_Q:
                            gated(BLK_Q - 1)
                        elif p % CHUNKS == 2 and p > CHUNKS:
                            gated(p // CHUNKS - 1)
                    if experts:
                        if 2 <= p < len(PHASES) + 2 and PHASES[p - 2][0] == "g":
                            expert_gate(PHASES[p - 2][1])
                        if 2 <= p < len(PHASES) + 2 and PHASES[p - 2][0] == "u":
                            expert_up(PHASES[p - 2][1])

            def finish(be):
                ve.wait_ge(S["moe_done"], be + 1)
                for t in range(TT):
                    V.tensor_tensor(x2[:, t, :], x2[:, t, :], acc[t][:, :], ALU.add).then_inc(S["fin_done"], 1)

            class Quant:

                def __init__(self, b, layer):
                    self.b, self.layer, self.r = b, layer, 2 * b + layer
                    self.x, self.w, self.wT = ((x1n, guw, guwT), (act, dnw, dnwT))[layer]
                    self.width = (D, INT)[layer]
                    self.kt = self.width // P

                def link(self, first):
                    before = sum(QUANT_LINKS[0]) if self.layer else 0
                    return Chain(ve, "linkX", sum(map(sum, QUANT_LINKS)) * self.b + before
                                 + sum(QUANT_LINKS[self.layer][:first]))

                def smoothing(self):
                    kt, link = self.kt, self.link(0)
                    ve.wait_ge(S["xw_in"], 64 * (self.b + 1))
                    for k in range(kt):
                        link.mark(V.tensor_reduce(col[:, 1, k:k + 1], self.wT[:, k, :], AX.X, ALU.max,
                                                  apply_absolute_value=True))
                    if self.layer == 0:
                        ve.wait_ge(S["tr_done"], 2 * self.b + 1)
                    else:
                        ve.wait_ge(S["xc_ps"], self.b + 1)
                    for k in range(kt):
                        link.mark(V.tensor_reduce(col[:, 0, k:k + 1], acc[k][:, :], AX.X, ALU.max,
                                                  apply_absolute_value=True))
                    link.wait()
                    link(V.tensor_scalar(col[:, 0:2, 0:kt], col[:, 0:2, 0:kt], EPS_Q, None, ALU.max))
                    link(V.reciprocal(col[:, 2, 0:kt], col[:, 1, 0:kt]))
                    V.tensor_tensor(col[:, 3, 0:kt], col[:, 0, 0:kt], col[:, 2, 0:kt], ALU.mult
                                    ).then_inc(S["s_arg"], 1)
                    ve.wait_ge(S["s_pow"], self.r + 1)
                    link(V.tensor_scalar(col[:, 5, 0:kt], col[:, 4, 0:kt], EPS_Q, None, ALU.max))
                    link(V.reciprocal(col[:, 6, 0:kt], col[:, 5, 0:kt]))
                    for d0, row in ((0, 5), (4, 6)):
                        for k in range(kt):
                            V.tensor_scalar(dg[:, d0 + k, :], ident[:], col[:, row, k:k + 1], None, ALU.mult
                                            ).then_inc(S["diag_ready"], 1)
                    assert link.n == QUANT_LINKS[self.layer][0], ("smoothing", link.n)

                def row_scales(self):
                    link = self.link(1)
                    ve.wait_ge(S["sbc_ps"], self.r + 1)
                    for src, row, r0 in ((self.w, acc[0], TT), (self.x, acc[1], 0)):
                        for t in range(TT):
                            link.mark(V.tensor_tensor(src[:, t, :], src[:, t, :], row[:, 0:self.width], ALU.mult))
                        link.wait()
                        for t in range(TT):
                            link.mark(V.tensor_reduce(rr[:, 0, r0 + t:r0 + t + 1], src[:, t, :], AX.X, ALU.max,
                                                      apply_absolute_value=True))
                    link.wait()
                    link(V.tensor_scalar(rr[:, 1, :], rr[:, 0, :], EPS_Q, 1.0 / QMAX, ALU.max, ALU.mult))
                    V.reciprocal(rr[:, 2, :], rr[:, 1, :]).then_inc(S["rinv_ready"], 1)
                    for t in range(TT):
                        V.tensor_scalar(dg[:, t, :], ident[:], rr[:, 1, TT + t:TT + t + 1], None, ALU.mult
                                        ).then_inc(S["wdiag_ready"], 1)
                    assert link.n == QUANT_LINKS[self.layer][1], ("row_scales", link.n)

                def integers(self):
                    for i in range(2 * TT):
                        ve.wait_ge(S["mg_ready"], 2 * TT * self.r + i + 1)
                        src, o = (self.x if i < TT else self.w)[:, i % TT, :], (i % TT) * self.width
                        V.tensor_scalar(q_rows[i // TT][:, o:o + self.width], src, MAGIC, QMAX,
                                        ALU.subtract, ALU.min).then_inc(S["q_ready"], 1)

                def transposed(self):
                    for i in range(2):
                        ve.wait_ge(S["qT_ps"], 2 * self.r + i + 1)
                        for k in range(0, self.kt, 2):
                            ins = V.tensor_scalar(q_cols[i][:, k * T:(k + 2) * T], accb[2 * i + k // 2][:, :],
                                                  -QMAX, None, ALU.max)
                        ins.then_inc(S["qT_ready"], 1)

                def scaled(self, t, ready):
                    ve.wait_ge(S["lin_ps"], TT * self.r + t + 1)
                    V.scalar_tensor_tensor(out=x1n[:, t, :], in0=acc[t][:, :], scalar=rr[:, 1, t:t + 1], in1=wsc,
                                           op0=ALU.mult, op1=ALU.mult).then_inc(S[ready], 1)

            def residual(b):
                ve.wait_ge(S["o_used"], NBLK * (b + 1))
                ve.wait_ge(S["x_res"], 16 * (b + 1))
                wait(ve, "out_done", 16 * b)
                for t in range(TT):
                    V.tensor_tensor(x2[:, t, :], x1n[:, t, :], acc[t][:, :], ALU.add).then_inc(S["linkO"], 1)

            def mlp_step(b, k):
                link_o = TT * 4 * b
                q = Quant(b, 0 if k < 7 else 1)
                if k == 0:
                    ve.wait_ge(S["linkO"], link_o + TT)
                    norm_stats(2 * b, x2, st, mv, "var_ready", Chain(ve, "linkLN", LINKS["LN"] * 2 * b))
                elif k in (1, 12):
                    norm_apply(2 * b + k // 12, x2, x1n, mv, rstd, "var_ready", "rstd_ready", "xn_ready")
                elif k in (2, 7):
                    q.smoothing()
                elif k in (3, 8):
                    q.row_scales()
                elif k in (4, 9):
                    q.integers()
                elif k in (5, 10):
                    q.transposed()
                elif k == 6:
                    ve.wait_ge(S["wsc_ready"], q.r + 1)
                    for t in range(TT):
                        q.scaled(t, "h_ready")
                    for t in range(TT):
                        ve.wait_ge(S["hth_ready"], TT * b + t + 1)
                        V.scalar_tensor_tensor(out=act[:, t, :], in0=hth[:, t, :], scalar=1.0, in1=x1n[:, t, 0:INT],
                                               op0=ALU.add, op1=ALU.mult).then_inc(S["linkO"], 1)
                    for t in range(TT):
                        ve.wait_ge(S["linkO"], link_o + TT + t + 1)
                        V.scalar_tensor_tensor(out=act[:, t, :], in0=act[:, t, :], scalar=0.5, in1=x1n[:, t, INT:D],
                                               op0=ALU.mult, op1=ALU.mult).then_inc(S["a_ready"], 1)
                elif k == 11:
                    ve.wait_ge(S["wsc_ready"], q.r + 1)
                    for t in range(TT):
                        q.scaled(t, "linkO")
                    for t in range(TT):
                        ve.wait_ge(S["linkO"], link_o + 2 * TT + t + 1)
                        V.tensor_tensor(x2[:, t, :], x2[:, t, :], x1n[:, t, :], ALU.add).then_inc(S["linkO"], 1)
                    ve.wait_ge(S["linkO"], link_o + 4 * TT)
                    norm_stats(2 * b + 1, x2, st, mv, "var_ready", Chain(ve, "linkLN", LINKS["LN"] * (2 * b + 1)))
                elif k == 14:
                    router(b)

            def router(b):
                link = Chain(ve, "linkG", LINKS["G"] * b)
                ve.wait_ge(S["lg_ps"], b + 1)
                link(V.tensor_copy(lg, acc[0][:, 0:TT * (NE + 1)].rearrange("p (t e) -> p t e", t=TT)))
                link(V.tensor_reduce(gm[:, 0, :], lg[:, :, 0:NE], AX.X, ALU.max))

                def rows(ap):
                    return ap.rearrange("p (t o) -> p t o", o=1).broadcast_to([P, TT, NE])

                V.tensor_tensor(pr[:, 0, :, :], lg[:, :, 0:NE], rows(gm[:, 0, :]), ALU.subtract
                                ).then_inc(S["ex_arg"], 1)
                ve.wait_ge(S["ex_ready"], b + 1)
                link(V.tensor_reduce(gm[:, 1, :], pr[:, 0, :, :], AX.X, ALU.add))
                link(V.reciprocal(gm[:, 2, :], gm[:, 1, :]))
                link.mark(V.tensor_tensor(pr[:, 0, :, :], pr[:, 0, :, :], rows(gm[:, 2, :]), ALU.mult))
                link.wait()
                carrier()
                for t in range(TT):
                    link.mark(V.max(top[:, t, :], pr[:, 0, t, :]))
                link.wait()
                carrier()
                for t in range(TT):
                    link.mark(V.max_index(topi[:, t, :], top[:, t, :], pr[:, 0, t, :]))
                link.wait()
                link(V.tensor_copy(topf[:, 0, :, :], topi[:, :, 0:2]))
                link(V.tensor_tensor(gm[:, 4, :], top[:, :, 0], top[:, :, 1], ALU.add))
                link(V.reciprocal(gm[:, 5, :], gm[:, 4, :]))
                link(V.scalar_tensor_tensor(out=topf[:, 1, :, :], in0=top[:, :, 0:2], scalar=0.5,
                                            in1=gm[:, 5, :].rearrange("p (t o) -> p t o", o=1).broadcast_to([P, TT, 2]),
                                            op0=ALU.mult, op1=ALU.mult))
                for i in range(2):
                    link(V.tensor_tensor(pr[:, 1 + i, :, :],
                                         iota[:, :].rearrange("p (o e) -> p o e", o=1).broadcast_to([P, TT, NE]),
                                         rows(topf[:, 0, :, i]), ALU.is_equal))
                    link(V.tensor_tensor(pr[:, 1 + i, :, :], pr[:, 1 + i, :, :], rows(topf[:, 1, :, i]), ALU.mult))
                link(V.tensor_tensor(comb[:, :, 0:NE], pr[:, 1, :, :], pr[:, 2, :, :], ALU.add))
                link(V.tensor_scalar(gm[:, 3, :], gm[:, 3, :], 1.0, None, ALU.add))
                link(V.reciprocal(gm[:, 3, :], gm[:, 3, :]))
                V.tensor_scalar(comb[:, :, NE], gm[:, 3, :], 0.5, None, ALU.mult).then_inc(S["comb_ready"], 1)
                assert link.n == LINKS["G"], ("G", link.n)

            stage_a(0, False)
            with ve.Fori(0, STEPS) as jj:
                step(0, jj, True, False)
            residual(0)
            with ve.Fori(1, B) as b:
                stage_a(b, True)
                with ve.Fori(0, STEPS) as jj:
                    step(b, jj, True, True)
                finish(b - 1)
                residual(b)
            for k in range(len(SLOTS)):
                mlp_step(B - 1, k)
            with ve.Fori(0, STEPS) as jj:
                step(B, jj, False, True)
            finish(B - 1)

        @block.tensor
        def _(pe):
            mm = nc.tensor.matmul
            pe.wait_ge(S["const_in"], 16 * 7)
            pe.wait_ge(S["const_done"], 2)

            def norm_transposes(l, src, dst, xn_ready, done):
                for t in range(TT):
                    pe.wait_ge(S[xn_ready], TT * l + t + 1)
                    for k in range(KD):
                        ins = nc.tensor.transpose(dst[k][:, t * P:(t + 1) * P], src[:, t, k * P:(k + 1) * P], ident[:])
                ins.then_inc(S[done], 1)

            def stage_a(b, mlp):
                norm_transposes(b, xn, bank[4:8], "a_xn_ready", "a_tr_done")
                pe.wait_ge(S["xT_ready"], KD * (b + 1))
                used = 0
                freed = []
                seen_z = 0
                for kind, m in ITEMS:
                    freed.append({"xi": ("xpad_ready", NBLK * b + m + 1), "z": ("z_ready", NBLK * b + m + 1),
                                  "bc": ("bc_ready", b + 1), "dt": ("dt_ready", b + 1),
                                  "dl": ("relu_ready", NBLK * b + m + 1)}[kind])
                for n, (kind, m) in enumerate(ITEMS):
                    if mlp and n - 1 in SLOTS:
                        mlp_step(b - 1, SLOTS.index(n - 1))
                    ps = bank[4 + n % 4]
                    if n >= 4:
                        pe.wait_ge(S[freed[n - 4][0]], freed[n - 4][1])
                    if kind in ("xi", "z"):
                        pe.wait_ge(w_in_s[used % W_RING], 16 * (W_USES // W_RING * b + used // W_RING + 1))
                        for k in range(KD):
                            ins = mm(ps[:, :], wst[:, used % W_RING, k * P:(k + 1) * P], xT[:, k, :],
                                     start=(k == 0), stop=(k == KD - 1))
                        used += 1
                    elif kind == "bc":
                        pe.wait_ge(S["u_ready"], NBLK * (b + 1))
                        for k in range(NBLK):
                            ins = mm(ps[0:2 * NS, :], xpw[:, k, DTR:DTR + 2 * NS], u[:, k, :],
                                     start=(k == 0), stop=(k == NBLK - 1))
                    elif kind == "dt":
                        for k in range(NBLK):
                            ins = mm(ps[:, :], xpw[:, k, 0:DTR], u[:, k, :], start=(k == 0), stop=(k == NBLK - 1))
                    else:
                        pe.wait_ge(S["dt_ready"], b + 1)
                        ins = mm(ps[:, :], dtw[:, m * P:(m + 1) * P], dtT, start=True, stop=True)
                    ins.then_inc(S["a_ps"], 1)
                pe.wait_ge(S["z_ready"], NBLK * (b + 1))

            def step(b, jj, scan, experts):
                q = STEPS * b + jj
                qe = STEPS * (b - 1) + jj

                def nsum(c):
                    jl, s = c // CHUNKS, c % 4
                    pe.wait_ge(S["hs_ready"], CREDIT + CH_Q * q + c + 1)
                    if c % CHUNKS == 0:
                        pe.wait_ge(S["y_done"], 2 + BLK_Q * q + jl - 1)
                    mm(Y[jl % 2][:, :], ident[:], pairs[:, s, :], start=(c % CHUNKS == 0),
                       stop=(c % CHUNKS == CHUNKS - 1)).then_inc(S["nsum_done"], 1)

                def phase(kind, i):
                    sl = i % SLOTS_E
                    if kind == "g":
                        pe.wait_ge(ew_up[sl], 16 * (EXP_Q // SLOTS_E * qe + i // SLOTS_E + 1))
                        pe.wait_ge(S["t1_done"], ONE + EXP_Q * qe + i)
                    if kind == "u":
                        pe.wait_ge(S["t2_done"], ONE + EXP_Q * qe + i)
                    if kind in "gu":
                        o = 0 if kind == "g" else D
                        for k in range(KD):
                            ins = mm((G if kind == "g" else U)[:, :], ew[:, sl, o + k * P:o + (k + 1) * P], x3T[:, k, :],
                                     start=(k == 0), stop=(k == KD - 1))
                        ins.then_inc(S["g_done" if kind == "g" else "u_done"], 1)
                    else:
                        pe.wait_ge(S["hm_ready"], ONE + EXP_Q * qe + i + 1)
                        pe.wait_ge(ew_down[sl], 32 * (EXP_Q // SLOTS_E * qe + i // SLOTS_E + 1))
                        for t in range(TT):
                            ins = mm(acc[t][:, :], hm[:, i % 2, t * P:(t + 1) * P], ew[:, sl, 2 * D:3 * D],
                                     start=False, stop=False, skip_group_check=True)
                        ins.then_inc(S["down_done"], 1)

                for p in range(CH_Q):
                    if experts and p < len(PHASES):
                        phase(*PHASES[p])
                    if scan:
                        nsum(p)

            def experts_begin(b):
                pe.wait_ge(S["x3_ready"], KD * b)
                pe.wait_ge(S["cT_ready"], b)
                for t in range(TT):
                    mm(acc[t][:, :], zerob[:], zeros4,
                       start=True, stop=False, skip_group_check=True)

            def experts_end():
                for t in range(TT):
                    ins = mm(acc[t][:, :], zerob[:], zeros4, start=False, stop=True, skip_group_check=True)
                ins.then_inc(S["moe_done"], 1)

            zeros4 = zerob[:, 0:P].rearrange("p (o c) -> p o c", o=1).broadcast_to([P, 4, P])

            def mlp_step(b, k):
                layer = 0 if k < 7 else 1
                r, kt = 2 * b + layer, (KD, 2)[layer]
                if k in (1, 12):
                    norm_transposes(2 * b + k // 12, x1n, acc, "xn_ready", "tr_done")
                elif k in (2, 7):
                    pe.wait_ge(S["diag_ready"], 2 * (KD + 2) * b + (2 * (KD + 2) if layer else 2 * KD))
                    for dst, d0 in ((acc[0], 0), (acc[1], 4)):
                        for i in range(kt):
                            ins = mm(dst[:, i * P:(i + 1) * P], ones[:], dg[:, d0 + i, :], start=True, stop=True)
                    ins.then_inc(S["sbc_ps"], 1)
                elif k in (3, 8):
                    pe.wait_ge(S["wdiag_ready"], TT * (r + 1))
                    for i in range(TT):
                        ins = mm(acc[2][:, i * P:(i + 1) * P], ones[:], dg[:, i, :], start=True, stop=True)
                    ins.then_inc(S["wsc_ps"], 1)
                elif k in (4, 9):
                    width = kt * P
                    for i in range(2):
                        if i == 1:
                            pe.wait_ge(S["wsc_ready"], r + 1)
                        for t in range(TT):
                            pe.wait_ge(S["q_ready"], 2 * TT * r + TT * i + t + 1)
                            for f in range(kt):
                                o = (f % 2) * T + t * P
                                ins = nc.tensor.transpose(accb[2 * i + f // 2][:, o:o + P],
                                                          q_rows[i][:, t * width + f * P:t * width + (f + 1) * P],
                                                          identb[:])
                        ins.then_inc(S["qT_ps"], 1)
                elif k in (5, 10):
                    pe.wait_ge(S["qT_ready"], 2 * r + 2)
                    for t in range(TT):
                        for f in range(kt):
                            ins = mm(acc[t][:, :], q_cols[0][:, f * T + t * P:f * T + (t + 1) * P],
                                     q_cols[1][:, f * T:(f + 1) * T], start=(f == 0), stop=(f == kt - 1))
                        ins.then_inc(S["lin_ps"], 1)
                elif k == 6:
                    for t in range(TT):
                        pe.wait_ge(S["a_ready"], TT * b + t + 1)
                        for f in range(INT // P):
                            ins = nc.tensor.transpose(acc[f][:, t * P:(t + 1) * P], act[:, t, f * P:(f + 1) * P],
                                                      ident[:])
                    ins.then_inc(S["xc_ps"], 1)
                elif k == 13:
                    pe.wait_ge(S["x3_ready"], KD * (b + 1))
                    for t in range(TT):
                        for f in range(KD):
                            ins = mm(acc[0][:, t * (NE + 1):(t + 1) * (NE + 1)], x3T[:, f, t * P:(t + 1) * P],
                                     gatew[:, f, :], start=(f == 0), stop=(f == KD - 1))
                    ins.then_inc(S["lg_ps"], 1)
                elif k == 14:
                    pe.wait_ge(S["comb_ready"], b + 1)
                    for t in range(TT):
                        ins = nc.tensor.transpose(acc[1][0:NE + 1, t * P:(t + 1) * P], comb[:, t, :], ident[:])
                    ins.then_inc(S["comb_ps"], 1)

            def mixer_out(b):
                wait(pe, "fin_done", TT * b)
                pe.wait_ge(S["y_done"], 2 + NBLK * (b + 1))
                for k in range(NBLK):
                    n = len(W_ITEMS) + k
                    pe.wait_ge(w_in_s[n % W_RING], 16 * (W_USES // W_RING * b + n // W_RING + 1))
                    for t in range(TT):
                        ins = mm(acc[t][:, :], zg[:, k, t * P:(t + 1) * P], wst[:, n % W_RING, :],
                                 start=(k == 0), stop=(k == NBLK - 1))
                    ins.then_inc(S["o_used"], 1)

            stage_a(0, False)
            with pe.Fori(0, STEPS) as jj:
                step(0, jj, True, False)
            mixer_out(0)
            with pe.Fori(1, B) as b:
                stage_a(b, True)
                experts_begin(b)
                with pe.Fori(0, STEPS) as jj:
                    step(b, jj, True, True)
                experts_end()
                mixer_out(b)
            for k in range(len(SLOTS)):
                mlp_step(B - 1, k)
            experts_begin(B)
            with pe.Fori(0, STEPS) as jj:
                step(B, jj, False, True)
            experts_end()


def kernel(**a):
    import concourse.bacc as bacc
    from concourse.bass_utils import run_bass_kernel_spmd as run

    a = {k: np.asarray(v) for k, v in a.items()}

    def blocks(w, rows):
        o, i = w.shape
        return np.ascontiguousarray(w.reshape(o // rows, rows, i // P, P).transpose(0, 3, 2, 1)).reshape(
            o // rows, P, (i // P) * rows)

    def cols(w):
        o, i = w.shape
        return np.ascontiguousarray(w.reshape(o, i // P, P).transpose(2, 1, 0))

    def tiles(v):
        return np.ascontiguousarray(v.reshape(v.shape[0] // P, P, -1).transpose(1, 0, 2))

    gu, dn = a["fside_BxS2xS2_0"], a["ctx_1024"]
    w1 = np.concatenate([a["L0_ffn_w1"], a["L0_ffn_ws_gate"].reshape(NSH, P, D)])
    w3 = np.concatenate([a["L0_ffn_w3"], a["L0_ffn_ws_up"].reshape(NSH, P, D)])
    w2 = np.concatenate([a["L0_ffn_w2"], a["L0_ffn_ws_down"].reshape(D, NSH, P).transpose(1, 0, 2)])
    up = [np.concatenate([blocks(w, P)[0] for w in ws])[None].reshape(NE + NSH, P, D) for ws in (w1, w3)]
    arrays = {
        "x": a["x"],
        "w_in": blocks(a["L0_attn_in_proj_weight"], P),
        "conv_w": tiles(a["L0_attn_conv1d_weight"].reshape(DI, TAPS)),
        "xp_w": cols(a["L0_attn_x_proj_weight"]),
        "dt_w": np.ascontiguousarray(a["L0_attn_dt_proj_weight"].T),
        "dt_b": tiles(a["L0_attn_dt_proj_bias"]).reshape(P, NBLK),
        "a_log": tiles(a["L0_attn_A_log"]),
        "d_skip": tiles(a["L0_attn_D"]).reshape(P, NBLK),
        "out_w": np.ascontiguousarray(a["L0_attn_out_proj_weight"].T).reshape(NBLK, P, D),
        "gu_w": np.stack([tiles(w) for w in gu]),
        "gu_wT": np.stack([cols(w) for w in gu]),
        "dn_w": np.stack([tiles(w) for w in dn]),
        "dn_wT": np.stack([cols(w) for w in dn]),
        "gate_w": cols(np.concatenate([a["L0_ffn_gate_w"], a["L0_ffn_shared_gate_w"]])),
        "exp_w": np.concatenate([up[0], up[1], np.ascontiguousarray(w2.transpose(0, 2, 1))], axis=2),
    }
    nc = bacc.Bacc("TRN2", target_bir_lowering=False, num_devices=1)
    args = {}
    for name, v in arrays.items():
        arrays[name] = np.ascontiguousarray(v)
        args[name] = nc.dram_tensor(f"in_{name}", v.shape, F32, kind="ExternalInput").ap()
    out = nc.dram_tensor("out_0", (B, T, D), F32, kind="ExternalOutput").ap()
    build(nc, out=out, **args)
    r = run(nc, [{f"in_{k}": v for k, v in arrays.items()}], core_ids=[0])
    return r.results[0]["out_0"]
```

```python
from contextlib import ExitStack

import numpy as np

import concourse.bass as bass
from concourse import mybir

F32 = mybir.dt.float32
BF16 = mybir.dt.bfloat16
U32 = mybir.dt.uint32
ALU = mybir.AluOpType
ACT = mybir.ActivationFunctionType
AX = mybir.AxisListType

P = 128
B = 4
T = 512
D = 512
DI = 1024
NS = 16
DTR = 128
TAPS = 4
INT = 256
NE = 16
NSH = 4
TT = T // P
KD = D // P
NBLK = DI // P
STEPS = 2
BLK_Q = NBLK // STEPS
EXP_Q = (NE + NSH) // STEPS
CN = 2
CHUNKS = NS // CN
CH_Q = BLK_Q * CHUNKS
W_RING = 4
SLOTS_E = 2
SHARED_Q = NSH // STEPS
EW = 2 * D + D
EPS_LN = 1e-5
EPS_Q = 1e-6
QMAX = 127.0
MAGIC = 1.5 * 2.0 ** 23
QUADS = CHUNKS // 2
QUAD_Q = CH_Q // 2
QUADS_V = 2
QUADS_P = QUAD_Q - QUADS_V
TWO = 2
CREDIT = 4
ONE = 1
DOWN_CREDIT = SLOTS_E

ITEMS = [("xi", m) for m in range(8)] + [("z", 0), ("z", 1), ("bc", 0), ("dt", 0)]
for _i in range(6):
    ITEMS += [("dl", _i), ("z", _i + 2)]
ITEMS += [("dl", 6), ("dl", 7)]
W_ITEMS = [it for it in ITEMS if it[0] in ("xi", "z")]
W_USES = len(W_ITEMS) + NBLK
PHASES = [("g", 0), ("u", 0)]
for _i in range(1, EXP_Q):
    PHASES += [("g", _i), ("u", _i), ("d", _i - 1)]
PHASES += [("d", EXP_Q - 1)]
MLP = [("stats0", 0), ("norm0", 1), ("reduce0", 3), ("diag0", 4), ("scales0", 5), ("integers0", 7),
       ("transposed0", 10), ("h", 11), ("act", 12), ("reduce1", 13), ("diag1", 14), ("scales1", 15),
       ("integers1", 16), ("transposed1", 18), ("sum", 19), ("norm1", 20), ("x3", 21), ("logits", 22),
       ("router", 24)]
PE_BEHIND = 3
GATE_BEHIND = 5
NSUM_BEHIND = 2
LINKS = {"A": 42, "LN": 8, "G": (2, 22)}
QUANT_LINKS = ((4 + 4 + 2, 2, 17), (2 + 2 + 2, 2, 17))



def build(nc, x, w_in, conv_w, xp_w, dt_w, dt_b, a_log, d_skip, out_w, gu_w, gu_wT, dn_w, dn_wT, gate_w,
          exp_w, out):
    with ExitStack() as ctx:
        def sb(name, shape, dt=F32):
            return ctx.enter_context(nc.sbuf_tensor(name, shape, dt))

        def sem(name):
            return ctx.enter_context(nc.semaphore(name))

        bc_dram = nc.dram_tensor("bc_dram", (2 * NS, T), F32, kind="Internal").ap()
        comb_dram = nc.dram_tensor("comb_dram", (NE + 1, T), F32, kind="Internal").ap()

        ident = sb("ident", [P, P])
        identb = sb("identb", [P, P], BF16)
        ones = sb("ones", [P, P])
        zerob = sb("zerob", [P, P], BF16)
        magic = sb("magic", [P, 1])
        halfpow = sb("halfpow", [P, 2, TT])
        iota = sb("iota", [P, NE])
        A_sb = sb("A_sb", [P, NBLK, NS])
        cw = sb("cw", [P, NBLK, TAPS])
        dtb = sb("dtb", [P, NBLK])
        dsk = sb("dsk", [P, NBLK])
        xpw = sb("xpw", [P, NBLK, DTR + 2 * NS])
        dtw = sb("dtw", [P, DI])
        gatew = sb("gatew", [P, KD, NE + 1])
        wst = sb("wst", [P, W_RING, 512])
        ew = sb("ew", [P, SLOTS_E, EW])
        comb_bc = sb("comb_bc", [P, SLOTS_E, T])
        x2 = sb("x2", [P, TT, D])
        x3T = sb("x3T", [P, KD, T])
        delta = sb("delta", [P, NBLK, T])
        u = sb("u", [P, NBLK, T])
        zg = sb("zg", [P, NBLK, T])
        BB = sb("BB", [P, NS, T])
        CB = sb("CB", [P, NS, T])
        du = sb("du", [P, 1, T])
        work = sb("work", [P, 6144])
        pairs = sb("pairs", [P, 4, T])
        etm = sb("etm", [P, 2, T])
        hm = sb("hm", [P, 2, T])
        st = sb("st", [P, TT, 6])
        mv = sb("mv", [P, TT, 2])
        rstd = sb("rstd", [P, TT])
        col = sb("col", [P, 8, 4])
        rr = sb("rr", [P, 3, 2 * TT])
        dtT = hm[:, 0, :]
        bcS = hm[0:2 * NS, 1, :]

        dA = work[:, 0:2048].rearrange("p (s n t) -> p s n t", s=2, n=CN)
        dBu = work[:, 2048:6144].rearrange("p (s n t) -> p s n t", s=4, n=CN)
        xpad = work[:, 0:1030].rearrange("p (s t) -> p s t", s=2)
        xT = work[:, 2048:4096].rearrange("p (k t) -> p k t", k=KD)
        xn = work[:, 4096:6144].rearrange("p (k t) -> p k t", k=TT)
        a_st = work[:, 1040:1064].rearrange("p (t i) -> p t i", t=TT)
        a_mv = work[:, 1064:1072].rearrange("p (t i) -> p t i", t=TT)
        a_rstd = work[:, 1072:1076]
        guwT = BB[:, 0:4, :]
        guw = CB[:, 0:4, :]
        zb = BB[:, 4:8, :].rearrange("p a b -> p (a b)").bitcast(BF16)
        q_rows = [zb[:, 0:2048], zb[:, 2048:4096]]
        zb = CB[:, 4:8, :].rearrange("p a b -> p (a b)").bitcast(BF16)
        q_cols = [zb[:, 0:2048], zb[:, 2048:4096]]
        x1n = BB[:, 8:12, :]
        dnw = CB[:, 8:10, :].rearrange("p a (b i) -> p (a b) i", b=2)
        dnwT = CB[:, 10:12, :]
        hth = BB[:, 12:14, :].rearrange("p a (b i) -> p (a b) i", b=2)
        act = BB[:, 14:16, :].rearrange("p a (b i) -> p (a b) i", b=2)
        dg = CB[:, 12:14, :].rearrange("p a (b c) -> p (a b) c", b=4)
        wsc = CB[:, 14, :]
        cT = CB[0:NE + 1, 15, :]
        rt = CB[:, 12, :]
        lg = rt[:, 0:68].rearrange("p (t e) -> p t e", t=TT)
        comb = rt[:, 68:136].rearrange("p (t e) -> p t e", t=TT)
        pr = rt[:, 136:328].rearrange("p (i t e) -> p i t e", i=3, t=TT)
        top = rt[:, 328:360].rearrange("p (t e) -> p t e", t=TT)
        topi = rt[:, 360:392].bitcast(U32).rearrange("p (t e) -> p t e", t=TT)
        topf = rt[:, 392:408].rearrange("p (i t e) -> p i t e", i=2, t=TT)
        gm = rt[:, 408:432].rearrange("p (i t) -> p i t", i=6)
        sp_e, sp_err, sp_ln, sp_inv = (
            [work[:, o + i * T:o + (i + 1) * T] for o in (4096, 0)] for i in range(4))
        bank = [ctx.enter_context(nc.psum_tensor(f"bank{i}", [P, 512], F32)) for i in range(8)]
        acc = bank[0:4]
        accb = [t[:, :].bitcast(BF16) for t in acc]
        G, U = bank[4], bank[5]
        Y = [bank[6], bank[7]]

        S = {n: sem(n) for n in (
            "const_in a_var_ready a_rstd_ready a_xn_ready a_tr_done zero_done ident_done const_done "
            "a_exp x_in x_res var_ready rstd_ready xn_ready tr_done xT_ready a_ps xpad_ready "
            "conv_done th_ready u_ready z_ready bc_ready bc_out dt_ready delta_ready quad_ready "
            "quad_v_ready du_ready dbu_ready da_ready scan_done prod_done hs_ready nsum_done y_done "
            "g_done u_done eth_ready t1_done t2_done hm_ready down_done moe_done fin_done out_done "
            "o_used xw_in xc_ps s_arg s_pow diag_ready sbc_ps rinv_ready wdiag_ready mg_ready wsc_ps "
            "wsc_ready q_ready qT_ps qT_ready lin_ps h_ready hth_ready a_ready x3_ready lg_ps ex_arg "
            "ex_ready comb_ready comb_ps cT_ready comb_out init linkA linkAN linkLN linkX linkG linkO "
            "linkS linkSP sp_e_ready relu_ready sp_inv_ready sp_err_ready sum_ready").split()}
        w_in_s = [sem(f"w_in{i}") for i in range(W_RING)]
        ew_up = [sem(f"ew_up{i}") for i in range(SLOTS_E)]
        ew_down = [sem(f"ew_down{i}") for i in range(SLOTS_E)]
        bcast = [sem(f"bcast{i}") for i in range(4)]

        def wait(eng, name, value):
            s = S[name] if isinstance(name, str) else name
            if not isinstance(value, int) or value > 0:
                eng.wait_ge(s, value)

        class Chain:

            def __init__(self, eng, name, base):
                self.eng, self.sem, self.base, self.n = eng, S[name], base, 0

            def mark(self, ins):
                self.n += 1
                ins.then_inc(self.sem, 1)

            def wait(self):
                self.eng.wait_ge(self.sem, self.base + self.n)

            def __call__(self, ins):
                self.mark(ins)
                self.wait()

        def mlp_steps(step, b, item, behind):
            for name, slot in MLP:
                if min(slot + behind, len(ITEMS) - 1) == item:
                    step(b, name)

        def whole_mlp(step, b):
            for name, _ in MLP:
                step(b, name)

        block = ctx.enter_context(nc.Block())

        @block.sync
        def _(sp):
            for dst, src in ((cw, conv_w), (dtb, dt_b), (dsk, d_skip), (A_sb, a_log), (xpw, xp_w),
                             (dtw, dt_w), (gatew, gate_w)):
                sp.dma_start(dst[:], src).then_inc(S["const_in"], 16)

            def batch_x(b):
                return x[bass.ds(b, 1), :, :].rearrange("o (t p) d -> p (o t) d", p=P)

            def weight(b, n, src):
                m = n - W_RING
                if m < 0:
                    wait(sp, "o_used", NBLK * b + m + 1)
                elif m < len(W_ITEMS):
                    sp.wait_ge(S["a_ps"], len(ITEMS) * b + ITEMS.index(W_ITEMS[m]) + 1)
                else:
                    sp.wait_ge(S["o_used"], NBLK * b + m - len(W_ITEMS) + 1)
                sp.dma_start(wst[:, n % W_RING, :], src).then_inc(w_in_s[n % W_RING], 16)

            def load_x(b):
                wait(sp, "hs_ready", 0 if isinstance(b, int) else CREDIT + STEPS * CH_Q * b)
                sp.dma_start(xn, batch_x(b)).then_inc(S["x_in"], 16)

            def load_a(b):
                n = 0
                for kind, m in ITEMS:
                    if kind in ("xi", "z"):
                        weight(b, n, w_in[m + (NBLK if kind == "z" else 0)])
                        n += 1
                        if n == W_RING and not isinstance(b, int):
                            load_mlp(b - 1)
                    if (kind, m) == ("z", 5):
                        sp.wait_ge(S["bc_ready"], 1 + b)
                        sp.dma_start(bc_dram, bcS).then_inc(S["bc_out"], 16)
                        sp.wait_ge(S["bc_out"], 16 * b + 16)
                        wait(sp, "q_ready", 4 * TT * (b - 1) + 2 * TT)
                        broadcast(b, 0)
                wait(sp, "lin_ps", 2 * TT * b)
                broadcast(b, 1)
                wait(sp, "tr_done", 2 * b)
                broadcast(b, 2)
                if not isinstance(b, int):
                    comb_rows(b - 1)
                    sp.wait_ge(S["comb_out"], 16 * b)
                broadcast(b, 3)

            def broadcast(b, g):
                for half, dst in enumerate((BB, CB)):
                    rows = bc_dram[half * NS + 4 * g:half * NS + 4 * g + 4, :]
                    sp.dma_start(dst[:, 4 * g:4 * g + 4, :],
                                 rows.rearrange("n t -> (n t)").partition_broadcast(P)
                                 .rearrange("p (n t) -> p n t", n=4)).then_inc(bcast[g], 16)

            def load_e(be, jj):
                qe = STEPS * be + jj
                """An expert's gate and up weights when the slot's last expert is through with its own,
                its down weights and combine weights when that one's last product is made."""
                sp.wait_ge(S["comb_out"], 16 * be + 16)
                for i in range(EXP_Q):
                    routed = EXP_Q - SHARED_Q
                    e = jj * routed + i if i < routed else NE + jj * SHARED_Q + (i - routed)
                    src = exp_w[bass.ds(e, 1), :, :].rearrange("o p n -> p (o n)")
                    sp.wait_ge(S["u_done"], EXP_Q * qe + i + 1)
                    sp.dma_start(ew[:, i % SLOTS_E, 0:2 * D], src[:, 0:2 * D]).then_inc(ew_up[i % SLOTS_E], 16)
                    sp.wait_ge(S["down_done"], EXP_Q * qe + i + 1)
                    sp.dma_start(ew[:, i % SLOTS_E, 2 * D:3 * D], src[:, 2 * D:3 * D]).then_inc(ew_down[i % SLOTS_E], 16)
                    src = comb_dram[bass.ds(e, 1), :] if i < routed else comb_dram[NE:NE + 1, :]
                    sp.dma_start(comb_bc[:, i % SLOTS_E, :], src.rearrange("o t -> (o t)").partition_broadcast(P)
                                 ).then_inc(ew_down[i % SLOTS_E], 16)

            def load_res(b):
                sp.wait_ge(S["prod_done"], STEPS * CH_Q * (b + 1))
                sp.dma_start(x1n, batch_x(b)).then_inc(S["x_res"], 16)

            def load_o(b, ks):
                for k in ks:
                    weight(b, len(W_ITEMS) + k, out_w[k])

            def load_mlp(b):
                for dst, src in ((guwT, gu_wT), (guw, gu_w), (dnw, dn_w), (dnwT, dn_wT)):
                    sp.dma_start(dst, src[bass.ds(b, 1)].rearrange("o p k n -> p (o k) n")
                                 ).then_inc(S["xw_in"], 16)

            def comb_rows(b):
                sp.wait_ge(S["cT_ready"], b + 1)
                sp.dma_start(comb_dram, cT).then_inc(S["comb_out"], 16)

            load_x(0)
            load_a(0)
            load_o(0, range(W_RING))
            with sp.Fori(1, B) as b:
                load_x(b)
                load_res(b - 1)
                load_o(b - 1, range(W_RING, NBLK))
                load_a(b)
                load_o(b, range(W_RING))
                with sp.Fori(0, STEPS) as jj:
                    load_e(b - 1, jj)
            load_res(B - 1)
            load_mlp(B - 1)
            load_o(B - 1, range(W_RING, NBLK))
            comb_rows(B - 1)
            with sp.Fori(0, STEPS) as jj:
                load_e(B - 1, jj)
            sp.wait_ge(S["out_done"], ONE + 16 * B)

        @block.gpsimd
        def _(pool):
            nc.gpsimd.memset(ident[:], 0.0).then_inc(S["zero_done"], 1)
            nc.gpsimd.memset(ones[:], 1.0)
            nc.gpsimd.memset(zerob[:], 0.0)
            nc.gpsimd.memset(magic[:], MAGIC)
            nc.gpsimd.memset(halfpow[:, 0, :], 0.5)
            nc.gpsimd.memset(halfpow[:, 1, :], -0.5).then_inc(S["ident_done"], 1)
            pool.wait_ge(S["zero_done"], 1)
            nc.gpsimd.affine_select(out=ident[:], in_=ident[:], compare_op=ALU.not_equal, fill=1.0, base=0,
                                    pattern=[[-1, P]], channel_multiplier=1).then_inc(S["ident_done"], 1)
            pool.wait_ge(S["ident_done"], 2)
            nc.gpsimd.tensor_copy(identb[:], ident[:]).then_inc(S["const_done"], 1)
            nc.gpsimd.iota(iota[:], pattern=[[1, NE]], base=0, channel_multiplier=0,
                           allow_small_or_imprecise_dtypes=True).then_inc(S["const_done"], 1)

            def power(ready, value, dst, src, exponent, done):
                pool.wait_ge(S[ready], value)
                nc.gpsimd.tensor_tensor(dst, src, exponent, ALU.pow).then_inc(S[done], 1)

            def norm(l):
                power("var_ready", l + 1, rstd[:], mv[:, :, 1], halfpow[:, 1, :], "rstd_ready")

            def mlp_step(b, k):
                if k == "stats0":
                    norm(2 * b)
                elif k in ("reduce0", "reduce1"):
                    layer = int(k[-1])
                    kt = (KD, 2)[layer]
                    power("s_arg", 2 * b + layer + 1, col[:, 4, 0:kt], col[:, 3, 0:kt], halfpow[:, 0, 0:kt], "s_pow")
                elif k == "sum":
                    norm(2 * b + 1)

            def stage_a(b, mlp):
                power("a_var_ready", b + 1, a_rstd, a_mv[:, :, 1], halfpow[:, 1, :], "a_rstd_ready")
                for n, (kind, m) in enumerate(ITEMS):
                    if kind == "dl":
                        softplus(b, m)
                    if mlp:
                        mlp_steps(mlp_step, b - 1, n, 0)

            def step(b, jj, scan, experts):
                q = STEPS * b + jj
                qe = STEPS * (b - 1) + jj
                if scan:
                    pool.wait_ge(S["delta_ready"], NBLK * (b + 1))
                    pool.wait_ge(S["u_ready"], NBLK * (b + 1))
                    pool.wait_ge(S["a_ps"], len(ITEMS) * (b + 1))

                def chunk(c):
                    jl, s, n0 = c // CHUNKS, c % 4, CN * (c % CHUNKS)
                    if c % CHUNKS == 0:
                        dj = delta[:, bass.ds(jj * BLK_Q + jl, 1), :].rearrange("p o t -> p (o t)")
                        uj = u[:, bass.ds(jj * BLK_Q + jl, 1), :].rearrange("p o t -> p (o t)")
                        pool.wait_ge(S["dbu_ready"], ONE + CH_Q * q + c)
                        nc.gpsimd.tensor_tensor(du[:, 0, :], dj, uj, ALU.mult).then_inc(S["du_ready"], 1)
                        pool.wait_ge(S["du_ready"], BLK_Q * q + jl + 1)
                    pool.wait_ge(bcast[n0 // 4], 32 * (b + 1))
                    pool.wait_ge(S["hs_ready"], CREDIT + CH_Q * q + c - 3)
                    nc.gpsimd.tensor_tensor(
                        dBu[:, s, :, :], du[:, 0:1, :].broadcast_to([P, CN, T]),
                        BB[:, n0:n0 + CN, :], ALU.mult).then_inc(S["dbu_ready"], 1)

                def gate(i):
                    pool.wait_ge(S["t2_done"], ONE + EXP_Q * qe + i + 1)
                    pool.wait_ge(S["down_done"], EXP_Q * qe + i + 1)
                    pool.wait_ge(ew_down[i % SLOTS_E], 32 * (EXP_Q // SLOTS_E * qe + i // SLOTS_E + 1))
                    nc.gpsimd.tensor_tensor(hm[:, i % 2, :], etm[:, 1, :], comb_bc[:, i % SLOTS_E, :],
                                            ALU.mult).then_inc(S["hm_ready"], 1)

                def quad(c):
                    pool.wait_ge(S["hs_ready"], CREDIT + CH_Q * q + c + 1)
                    nc.gpsimd.tensor_tensor(pairs[:, c % 4 - 1, :], pairs[:, c % 4 - 1, :], pairs[:, c % 4, :],
                                            ALU.add).then_inc(S["quad_ready"], 1)

                for p in range(CH_Q):
                    if scan:
                        if experts and p >= 5 and p % 2 == 1:
                            quad(p - 4)
                        chunk(p)
                    if experts:
                        for n, (kind, i) in enumerate(PHASES):
                            if kind == "u" and min(n + GATE_BEHIND, CH_Q - 1) == p:
                                gate(i)

            def softplus(b, m):
                pool.wait_ge(S["sp_inv_ready"], NBLK * b + m + 1)
                nc.gpsimd.tensor_tensor(delta[:, m, :], delta[:, m, :], sp_ln[m % 2], ALU.add
                                        ).then_inc(S["sum_ready"], 1)
                pool.wait_ge(S["sum_ready"], NBLK * b + m + 1)
                pool.wait_ge(S["sp_err_ready"], NBLK * b + m + 1)
                nc.gpsimd.tensor_tensor(delta[:, m, :], delta[:, m, :], sp_err[m % 2], ALU.subtract
                                        ).then_inc(S["delta_ready"], 1)

            stage_a(0, False)
            with pool.Fori(0, STEPS) as jj:
                step(0, jj, True, False)
            with pool.Fori(1, B) as b:
                stage_a(b, True)
                with pool.Fori(0, STEPS) as jj:
                    step(b, jj, True, True)
            whole_mlp(mlp_step, B - 1)
            with pool.Fori(0, STEPS) as jj:
                step(B, jj, False, True)

        @block.scalar
        def _(sc):
            sc.wait_ge(S["const_in"], 16 * 7)
            nc.scalar.activation(A_sb[:], A_sb[:], ACT.Exp).then_inc(S["a_exp"], 1)

            def head(b):
                sc.wait_ge(S["a_tr_done"], b + 1)
                for k in range(2):
                    nc.scalar.copy(xT[:, k, :], bank[4 + k][:, :]).then_inc(S["xT_ready"], 1)

            def store(be):
                sc.wait_ge(S["fin_done"], ONE + TT * be + TT)
                sc.dma_start(out[bass.ds(be, 1), :, :].rearrange("o (t p) d -> p (o t) d", p=P), x2[:]
                             ).then_inc(S["out_done"], 16)

            def stage_a(b, mlp):

                def tanh_x(m):
                    sc.wait_ge(S["conv_done"], NBLK * b + m + 1)
                    if m >= 2:
                        sc.wait_ge(S["u_ready"], NBLK * b + m - 1)
                    nc.scalar.activation(etm[:, m % 2, :], u[:, m, :], ACT.Tanh).then_inc(S["th_ready"], 1)

                for n, (kind, m) in enumerate(ITEMS):
                    sc.wait_ge(S["a_ps"], len(ITEMS) * b + n + 1)
                    ps = bank[4 + n % 4]
                    if kind == "xi":
                        if m >= 2:
                            sc.wait_ge(S["conv_done"], NBLK * b + m - 1)
                        nc.scalar.copy(xpad[:, m % 2, TAPS - 1:TAPS - 1 + T], ps[:, :]).then_inc(S["xpad_ready"], 1)
                        if m >= 1:
                            tanh_x(m - 1)
                    elif kind == "z":
                        if m == 0:
                            tanh_x(NBLK - 1)
                            sc.wait_ge(S["u_ready"], NBLK * b + NBLK - 1)
                        elif m == 1:
                            sc.wait_ge(S["u_ready"], NBLK * b + NBLK)
                        else:
                            sc.wait_ge(S["z_ready"], NBLK * b + m - 1)
                        nc.scalar.activation(etm[:, m % 2, :], ps[:, :], ACT.Tanh, scale=0.5
                                             ).then_inc(S["th_ready"], 1)
                    elif kind == "bc":
                        nc.scalar.copy(bcS, ps[0:2 * NS, :]).then_inc(S["bc_ready"], 1)
                    elif kind == "dt":
                        nc.scalar.copy(dtT, ps[:, :]).then_inc(S["dt_ready"], 1)
                    else:
                        s = m % 2
                        if m < 2:
                            sc.wait_ge(S["conv_done"], NBLK * (b + 1))
                        else:
                            sc.wait_ge(S["delta_ready"], NBLK * b + m - 1)
                        nc.scalar.activation(sp_e[s], ps[:, :], ACT.Abs, bias=dtb[:, m:m + 1]
                                             ).then_inc(S["linkSP"], 1)
                        sc.wait_ge(S["linkSP"], 2 * (NBLK * b + m) + 1)
                        nc.scalar.activation(sp_e[s], sp_e[s], ACT.Exp, scale=-1.0).then_inc(S["sp_e_ready"], 1)
                        sc.wait_ge(S["sp_e_ready"], NBLK * b + m + 1)
                        nc.scalar.activation(sp_ln[s], sp_e[s], ACT.Ln, bias=ones[:, 0:1]).then_inc(S["linkSP"], 1)
                        nc.scalar.activation(delta[:, m, :], ps[:, :], ACT.Relu, bias=dtb[:, m:m + 1]
                                             ).then_inc(S["relu_ready"], 1)
                        sc.wait_ge(S["linkSP"], 2 * (NBLK * b + m) + 2)
                        nc.scalar.activation(sp_inv[s], sp_ln[s], ACT.Exp, scale=-1.0
                                             ).then_inc(S["sp_inv_ready"], 1)
                    if mlp:
                        mlp_steps(mlp_step, b - 1, n, 1)

            def step(b, jj, scan, experts):
                q = STEPS * b + jj
                qe = STEPS * (b - 1) + jj
                if scan:
                    sc.wait_ge(S["delta_ready"], NBLK * (b + 1))

                def chunk(c):
                    jl, s, n0 = c // CHUNKS, c % 2, CN * (c % CHUNKS)
                    dj = delta[:, bass.ds(jj * BLK_Q + jl, 1), 1:T].rearrange("p o t -> p (o t)")
                    sc.wait_ge(S["scan_done"], 2 + CH_Q * q + c - 1)
                    for i in range(CN):
                        a = A_sb[:, bass.ds(jj * BLK_Q + jl, 1), n0 + i:n0 + i + 1].rearrange("p o n -> p (o n)")
                        ins = nc.scalar.activation(dA[:, s, i, 1:T], dj, ACT.Exp, scale=a)
                    ins.then_inc(S["da_ready"], 1)

                def tanh_g(i):
                    sc.wait_ge(S["g_done"], EXP_Q * qe + i + 1)
                    sc.wait_ge(S["t1_done"], ONE + EXP_Q * qe + i)
                    nc.scalar.activation(etm[:, 0, :], G[:, :], ACT.Tanh, scale=0.5).then_inc(S["eth_ready"], 1)

                for p in range(CH_Q):
                    if scan:
                        chunk(p)
                    if experts and p >= 1 and p - 1 < len(PHASES) and PHASES[p - 1][0] == "g":
                        tanh_g(PHASES[p - 1][1])

            def magic_rows(b, layer, src_x, src_w):
                sc.wait_ge(S["rinv_ready"], 2 * b + layer + 1)
                for i in range(2 * TT):
                    src = (src_x if i < TT else src_w)[:, i % TT, :]
                    nc.scalar.activation(src, src, ACT.Identity, scale=rr[:, 2, i:i + 1], bias=magic[:, 0:1]
                                         ).then_inc(S["mg_ready"], 1)

            def weight_scales(b, layer):
                sc.wait_ge(S["wsc_ps"], 2 * b + layer + 1)
                nc.scalar.copy(wsc, acc[2][:, :]).then_inc(S["wsc_ready"], 1)

            def mlp_step(b, k):
                if k == "scales0":
                    magic_rows(b, 0, x1n, guw)
                elif k == "integers0":
                    weight_scales(b, 0)
                elif k == "h":
                    for t in range(TT):
                        sc.wait_ge(S["h_ready"], TT * b + t + 1)
                        nc.scalar.activation(hth[:, t, :], x1n[:, t, 0:INT], ACT.Tanh, scale=0.5
                                             ).then_inc(S["hth_ready"], 1)
                elif k == "scales1":
                    magic_rows(b, 1, act, dnw)
                elif k == "integers1":
                    weight_scales(b, 1)
                elif k == "x3":
                    sc.wait_ge(S["tr_done"], 2 * b + 2)
                    for i in range(KD):
                        nc.scalar.copy(x3T[:, i, :], acc[i][:, :]).then_inc(S["x3_ready"], 1)
                elif k == "logits":
                    sc.wait_ge(S["ex_arg"], b + 1)
                    nc.scalar.activation(pr[:, 0, :, :], pr[:, 0, :, :], ACT.Exp)
                    nc.scalar.activation(gm[:, 3, :], lg[:, :, NE], ACT.Exp, scale=-1.0).then_inc(S["ex_ready"], 1)

            def combine_rows(b):
                sc.wait_ge(S["comb_ps"], b + 1)
                nc.scalar.copy(cT, acc[1][0:NE + 1, :]).then_inc(S["cT_ready"], 1)

            head(0)
            stage_a(0, False)
            with sc.Fori(0, STEPS) as jj:
                step(0, jj, True, False)
            with sc.Fori(1, B) as b:
                head(b)
                stage_a(b, True)
                combine_rows(b - 1)
                with sc.Fori(0, STEPS) as jj:
                    step(b, jj, True, True)
                store(b - 1)
            whole_mlp(mlp_step, B - 1)
            combine_rows(B - 1)
            with sc.Fori(0, STEPS) as jj:
                step(B, jj, False, True)
            store(B - 1)

        @block.vector
        def _(ve):
            V = nc.vector
            for i, (free, n) in enumerate((("scan_done", 2), ("y_done", 2), ("hs_ready", CREDIT), ("nsum_done", TWO),
                                           ("t1_done", ONE), ("t2_done", ONE), ("hm_ready", ONE),
                                           ("dbu_ready", ONE), ("u_done", DOWN_CREDIT), ("down_done", DOWN_CREDIT),
                                           ("fin_done", ONE), ("out_done", ONE))):
                V.memset(comb_bc[:, 0, i:i + 1], 0.0).then_inc(S[free], n)
            ve.wait_ge(S["const_in"], 16 * 7)
            V.tensor_scalar(cw[:], cw[:], 0.5, None, ALU.mult).then_inc(S["init"], 1)
            ve.wait_ge(S["a_exp"], 1)
            V.tensor_scalar(A_sb[:], A_sb[:], -1.0, None, ALU.mult).then_inc(S["init"], 1)
            ve.wait_ge(S["init"], 2)
            ve.wait_ge(S["const_done"], 2)

            def carrier():
                V.memset(rr[:, 0, 0:1], 0.0)

            def norm_stats(l, src, st, mv, var_ready, link):
                for t in range(TT):
                    link.mark(V.bn_stats(st[:, t, :], src[:, t, :]))
                link.wait()
                carrier()
                for t in range(TT):
                    link.mark(V.bn_aggr(mv[:, t, :], st[:, t, :]))
                link.wait()
                V.tensor_scalar(mv[:, :, 1], mv[:, :, 1], EPS_LN, None, ALU.add).then_inc(S[var_ready], 1)
                assert link.n == LINKS["LN"], ("LN", link.n)

            def norm_apply(l, src, dst, mv, rstd, var_ready, rstd_ready, xn_ready):
                ve.wait_ge(S[rstd_ready], l + 1)
                ve.wait_ge(S[var_ready], l + 1)
                for t in range(TT):
                    V.tensor_scalar(dst[:, t, :], src[:, t, :], mv[:, t, 0:1], rstd[:, t:t + 1],
                                    ALU.subtract, ALU.mult).then_inc(S[xn_ready], 1)

            def head(b):
                link = Chain(ve, "linkA", LINKS["A"] * b)
                ve.wait_ge(S["x_in"], 16 * (b + 1))
                norm_stats(b, xn, a_st, a_mv, "a_var_ready", Chain(ve, "linkAN", LINKS["LN"] * b))
                norm_apply(b, xn, xn, a_mv, a_rstd, "a_var_ready", "a_rstd_ready", "a_xn_ready")
                link(V.memset(xpad[:, :, 0:TAPS - 1], 0.0))
                ve.wait_ge(S["a_tr_done"], b + 1)
                for k in range(2, KD):
                    V.tensor_copy(xT[:, k, :], bank[4 + k][:, :]).then_inc(S["xT_ready"], 1)

            def stage_a(b, mlp):
                link = Chain(ve, "linkA", LINKS["A"] * b)
                link.n = 1

                def conv(m):
                    xp = xpad[:, m % 2, :]
                    ve.wait_ge(S["xpad_ready"], NBLK * b + m + 1)
                    link(V.tensor_scalar(u[:, m, :], xp[:, 0:T], cw[:, m, 0:1], None, ALU.mult))
                    for j in range(1, TAPS):
                        ins = V.scalar_tensor_tensor(out=u[:, m, :], in0=xp[:, j:j + T], scalar=cw[:, m, j:j + 1],
                                                     in1=u[:, m, :], op0=ALU.mult, op1=ALU.add)
                        if j < TAPS - 1:
                            link(ins)
                    ins.then_inc(S["conv_done"], 1)

                def silu_x(m):
                    ve.wait_ge(S["th_ready"], 2 * NBLK * b + m + 1)
                    V.scalar_tensor_tensor(out=u[:, m, :], in0=etm[:, m % 2, :], scalar=1.0, in1=u[:, m, :],
                                           op0=ALU.add, op1=ALU.mult).then_inc(S["u_ready"], 1)

                def silu_z(m, n):
                    ve.wait_ge(S["th_ready"], 2 * NBLK * b + NBLK + m + 1)
                    V.scalar_tensor_tensor(out=zg[:, m, :], in0=etm[:, m % 2, :], scalar=1.0,
                                           in1=bank[4 + n % 4][:, :], op0=ALU.add, op1=ALU.mult
                                           ).then_inc(S["z_ready"], 1)

                def softplus(m):
                    s = m % 2
                    ve.wait_ge(S["sp_e_ready"], NBLK * b + m + 1)
                    link(V.tensor_scalar(sp_err[s], sp_e[s], 1.0, -1.0, ALU.add, ALU.add))
                    link(V.tensor_tensor(sp_err[s], sp_err[s], sp_e[s], ALU.subtract))
                    ve.wait_ge(S["sp_inv_ready"], NBLK * b + m + 1)
                    V.tensor_tensor(sp_err[s], sp_err[s], sp_inv[s], ALU.mult).then_inc(S["sp_err_ready"], 1)

                for n, (kind, m) in enumerate(ITEMS):
                    if kind == "xi":
                        conv(m)
                        if m >= 1:
                            silu_x(m - 1)
                    elif kind == "z":
                        if m == 0:
                            silu_x(NBLK - 1)
                        silu_z(m, n)
                    elif kind == "dl":
                        softplus(m)
                    if mlp:
                        mlp_steps(mlp_step, b - 1, n, 0)
                ve.wait_ge(S["delta_ready"], NBLK * (b + 1))
                link.mark(V.memset(dA[:, :, :, 0:1], 0.0))
                assert link.n == LINKS["A"], ("A", link.n)

            def step(b, jj, scan, experts):
                q = STEPS * b + jj
                qe = STEPS * (b - 1) + jj

                if scan:
                    ve.wait_ge(S["linkA"], LINKS["A"] * (b + 1))

                def scan_chunk(c):
                    s = c % 4
                    ve.wait_ge(S["da_ready"], CH_Q * q + c + 1)
                    ve.wait_ge(S["dbu_ready"], ONE + CH_Q * q + c + 1)
                    state = dBu[:, s, :, :].rearrange("p n t -> p (n t)")
                    V.tensor_tensor_scan(state, dA[:, c % 2, :, :].rearrange("p n t -> p (n t)"), state,
                                         0.0, ALU.mult, ALU.add).then_inc(S["scan_done"], 1)

                def product(c):
                    s, n0 = c % 4, CN * (c % CHUNKS)
                    ve.wait_ge(S["scan_done"], 2 + CH_Q * q + c + 1)
                    ve.wait_ge(bcast[n0 // 4], 32 * (b + 1))
                    V.tensor_tensor(dBu[:, s, :, :], dBu[:, s, :, :], CB[:, n0:n0 + CN, :], ALU.mult
                                    ).then_inc(S["prod_done"], 1)

                def pair_sum(c):
                    s = c % 4
                    ve.wait_ge(S["prod_done"], CH_Q * q + c + 1)
                    ve.wait_ge(S["nsum_done"], TWO + QUAD_Q * (q - STEPS) + c // 2 - 1)
                    V.tensor_tensor(pairs[:, s, :], dBu[:, s, 0, :], dBu[:, s, 1, :], ALU.add
                                    ).then_inc(S["hs_ready"], 1)

                def quad(c):
                    ve.wait_ge(S["hs_ready"], CREDIT + CH_Q * q + c + 1)
                    V.tensor_tensor(pairs[:, c % 4 - 1, :], pairs[:, c % 4 - 1, :], pairs[:, c % 4, :], ALU.add
                                    ).then_inc(S["quad_v_ready"], 1)

                def gated(jl):
                    ujl = u[:, bass.ds(jj * BLK_Q + jl, 1), :].rearrange("p o t -> p (o t)")
                    zjl = zg[:, bass.ds(jj * BLK_Q + jl, 1), :].rearrange("p o t -> p (o t)")
                    djl = dsk[:, bass.ds(jj * BLK_Q + jl, 1)]
                    if experts:
                        ve.wait_ge(S["nsum_done"], TWO + QUAD_Q * (q - STEPS) + QUADS * (jl + 1))
                    else:
                        ve.wait_ge(S["hs_ready"], CREDIT + CH_Q * q + CHUNKS * (jl + 1))
                    V.scalar_tensor_tensor(out=ujl, in0=ujl, scalar=djl, in1=Y[jl % 2][:, :], op0=ALU.mult,
                                           op1=ALU.add).then_inc(S["linkS"], 1)
                    ve.wait_ge(S["linkS"], BLK_Q * q + jl + 1)
                    V.scalar_tensor_tensor(out=zjl, in0=ujl, scalar=0.5, in1=zjl, op0=ALU.mult, op1=ALU.mult
                                           ).then_inc(S["y_done"], 1)

                def expert_gate(i):
                    ve.wait_ge(S["eth_ready"], EXP_Q * qe + i + 1)
                    ve.wait_ge(S["hm_ready"], ONE + EXP_Q * qe + i)
                    V.scalar_tensor_tensor(out=etm[:, 1, :], in0=etm[:, 0, :], scalar=1.0, in1=G[:, :],
                                           op0=ALU.add, op1=ALU.mult).then_inc(S["t1_done"], 1)

                def expert_up(i):
                    ve.wait_ge(S["u_done"], DOWN_CREDIT + EXP_Q * qe + i + 1)
                    ve.wait_ge(S["t1_done"], ONE + EXP_Q * qe + i + 1)
                    V.tensor_tensor(etm[:, 1, :], etm[:, 1, :], U[:, :], ALU.mult).then_inc(S["t2_done"], 1)

                for p in range(CH_Q + 1):
                    if scan:
                        if p < CH_Q:
                            scan_chunk(p)
                        if p >= 1 and experts:
                            pair_sum(p - 1)
                        if p < CH_Q:
                            product(p)
                        if experts and p == CH_Q - 1:
                            quad(CH_Q - 3)
                        if p == CH_Q:
                            if experts:
                                quad(CH_Q - 1)
                            gated(BLK_Q - 1)
                        elif p % CHUNKS == 4 and p > CHUNKS:
                            gated(p // CHUNKS - 1)
                    if experts:
                        if 2 <= p < len(PHASES) + 2 and PHASES[p - 2][0] == "g":
                            expert_gate(PHASES[p - 2][1])
                        if 2 <= p < len(PHASES) + 2 and PHASES[p - 2][0] == "u":
                            expert_up(PHASES[p - 2][1])

            def finish(be):
                ve.wait_ge(S["moe_done"], be + 1)
                for t in range(TT):
                    V.tensor_tensor(x2[:, t, :], x2[:, t, :], acc[t][:, :], ALU.add).then_inc(S["fin_done"], 1)

            class Quant:

                def __init__(self, b, layer):
                    self.b, self.layer, self.r = b, layer, 2 * b + layer
                    self.x, self.w, self.wT = ((x1n, guw, guwT), (act, dnw, dnwT))[layer]
                    self.width = (D, INT)[layer]
                    self.kt = self.width // P

                def link(self, first):
                    before = sum(QUANT_LINKS[0]) if self.layer else 0
                    return Chain(ve, "linkX", sum(map(sum, QUANT_LINKS)) * self.b + before
                                 + sum(QUANT_LINKS[self.layer][:first]))

                def reduce(self):
                    kt, link = self.kt, self.link(0)
                    ve.wait_ge(S["xw_in"], 64 * (self.b + 1))
                    for k in range(kt):
                        link.mark(V.tensor_reduce(col[:, 1, k:k + 1], self.wT[:, k, :], AX.X, ALU.max,
                                                  apply_absolute_value=True))
                    if self.layer == 0:
                        ve.wait_ge(S["tr_done"], 2 * self.b + 1)
                    else:
                        ve.wait_ge(S["xc_ps"], self.b + 1)
                    for k in range(kt):
                        link.mark(V.tensor_reduce(col[:, 0, k:k + 1], acc[k][:, :], AX.X, ALU.max,
                                                  apply_absolute_value=True))
                    link.wait()
                    link(V.tensor_scalar(col[:, 0:2, 0:kt], col[:, 0:2, 0:kt], EPS_Q, None, ALU.max))
                    link(V.reciprocal(col[:, 2, 0:kt], col[:, 1, 0:kt]))
                    V.tensor_tensor(col[:, 3, 0:kt], col[:, 0, 0:kt], col[:, 2, 0:kt], ALU.mult
                                    ).then_inc(S["s_arg"], 1)
                    assert link.n == QUANT_LINKS[self.layer][0], ("reduce", link.n)

                def diag(self):
                    kt, link = self.kt, self.link(1)
                    ve.wait_ge(S["s_pow"], self.r + 1)
                    link(V.tensor_scalar(col[:, 5, 0:kt], col[:, 4, 0:kt], EPS_Q, None, ALU.max))
                    link(V.reciprocal(col[:, 6, 0:kt], col[:, 5, 0:kt]))
                    for d0, row in ((0, 5), (4, 6)):
                        for k in range(kt):
                            V.tensor_scalar(dg[:, d0 + k, :], ident[:], col[:, row, k:k + 1], None, ALU.mult
                                            ).then_inc(S["diag_ready"], 1)
                    assert link.n == QUANT_LINKS[self.layer][1], ("diag", link.n)

                def scales(self):
                    link = self.link(2)
                    ve.wait_ge(S["sbc_ps"], self.r + 1)
                    for src, row, r0 in ((self.w, acc[0], TT), (self.x, acc[1], 0)):
                        for t in range(TT):
                            link.mark(V.tensor_tensor(src[:, t, :], src[:, t, :], row[:, 0:self.width], ALU.mult))
                        link.wait()
                        for t in range(TT):
                            link.mark(V.tensor_reduce(rr[:, 0, r0 + t:r0 + t + 1], src[:, t, :], AX.X, ALU.max,
                                                      apply_absolute_value=True))
                    link.wait()
                    link(V.tensor_scalar(rr[:, 1, :], rr[:, 0, :], EPS_Q, 1.0 / QMAX, ALU.max, ALU.mult))
                    V.reciprocal(rr[:, 2, :], rr[:, 1, :]).then_inc(S["rinv_ready"], 1)
                    for t in range(TT):
                        V.tensor_scalar(dg[:, t, :], ident[:], rr[:, 1, TT + t:TT + t + 1], None, ALU.mult
                                        ).then_inc(S["wdiag_ready"], 1)
                    assert link.n == QUANT_LINKS[self.layer][2], ("scales", link.n)

                def integers(self):
                    for i in range(2 * TT):
                        ve.wait_ge(S["mg_ready"], 2 * TT * self.r + i + 1)
                        src, o = (self.x if i < TT else self.w)[:, i % TT, :], (i % TT) * self.width
                        V.tensor_scalar(q_rows[i // TT][:, o:o + self.width], src, MAGIC, QMAX,
                                        ALU.subtract, ALU.min).then_inc(S["q_ready"], 1)

                def transposed(self):
                    for i in range(2):
                        ve.wait_ge(S["qT_ps"], 2 * self.r + i + 1)
                        for k in range(0, self.kt, 2):
                            ins = V.tensor_scalar(q_cols[i][:, k * T:(k + 2) * T], accb[2 * i + k // 2][:, :],
                                                  -QMAX, None, ALU.max)
                        ins.then_inc(S["qT_ready"], 1)

                def scaled(self, t, ready):
                    ve.wait_ge(S["lin_ps"], TT * self.r + t + 1)
                    V.scalar_tensor_tensor(out=x1n[:, t, :], in0=acc[t][:, :], scalar=rr[:, 1, t:t + 1], in1=wsc,
                                           op0=ALU.mult, op1=ALU.mult).then_inc(S[ready], 1)

            def residual(b):
                ve.wait_ge(S["o_used"], NBLK * (b + 1))
                ve.wait_ge(S["x_res"], 16 * (b + 1))
                ve.wait_ge(S["out_done"], ONE + 16 * b)
                for t in range(TT):
                    V.tensor_tensor(x2[:, t, :], x1n[:, t, :], acc[t][:, :], ALU.add).then_inc(S["linkO"], 1)

            def mlp_step(b, k):
                link_o = TT * 4 * b
                q = Quant(b, 1 if k.endswith("1") or k == "sum" else 0)
                if k == "stats0":
                    ve.wait_ge(S["linkO"], link_o + TT)
                    norm_stats(2 * b, x2, st, mv, "var_ready", Chain(ve, "linkLN", LINKS["LN"] * 2 * b))
                elif k in ("norm0", "norm1"):
                    norm_apply(2 * b + int(k[-1]), x2, x1n, mv, rstd, "var_ready", "rstd_ready", "xn_ready")
                elif k in ("reduce0", "reduce1"):
                    q.reduce()
                elif k in ("diag0", "diag1"):
                    q.diag()
                elif k in ("scales0", "scales1"):
                    q.scales()
                elif k in ("integers0", "integers1"):
                    q.integers()
                elif k in ("transposed0", "transposed1"):
                    q.transposed()
                elif k == "h":
                    ve.wait_ge(S["wsc_ready"], q.r + 1)
                    for t in range(TT):
                        q.scaled(t, "h_ready")
                elif k == "act":
                    for t in range(TT):
                        ve.wait_ge(S["hth_ready"], TT * b + t + 1)
                        V.scalar_tensor_tensor(out=act[:, t, :], in0=hth[:, t, :], scalar=1.0, in1=x1n[:, t, 0:INT],
                                               op0=ALU.add, op1=ALU.mult).then_inc(S["linkO"], 1)
                    for t in range(TT):
                        ve.wait_ge(S["linkO"], link_o + TT + t + 1)
                        V.scalar_tensor_tensor(out=act[:, t, :], in0=act[:, t, :], scalar=0.5, in1=x1n[:, t, INT:D],
                                               op0=ALU.mult, op1=ALU.mult).then_inc(S["a_ready"], 1)
                elif k == "sum":
                    ve.wait_ge(S["wsc_ready"], q.r + 1)
                    for t in range(TT):
                        q.scaled(t, "linkO")
                    for t in range(TT):
                        ve.wait_ge(S["linkO"], link_o + 2 * TT + t + 1)
                        V.tensor_tensor(x2[:, t, :], x2[:, t, :], x1n[:, t, :], ALU.add).then_inc(S["linkO"], 1)
                    ve.wait_ge(S["linkO"], link_o + 4 * TT)
                    norm_stats(2 * b + 1, x2, st, mv, "var_ready", Chain(ve, "linkLN", LINKS["LN"] * (2 * b + 1)))
                elif k == "logits":
                    logits(b)
                elif k == "router":
                    router(b)

            def rows(ap):
                return ap.rearrange("p (t o) -> p t o", o=1).broadcast_to([P, TT, NE])

            def logits(b):
                link = Chain(ve, "linkG", sum(LINKS["G"]) * b)
                ve.wait_ge(S["lg_ps"], b + 1)
                link(V.tensor_copy(lg, acc[0][:, 0:TT * (NE + 1)].rearrange("p (t e) -> p t e", t=TT)))
                link(V.tensor_reduce(gm[:, 0, :], lg[:, :, 0:NE], AX.X, ALU.max))

                V.tensor_tensor(pr[:, 0, :, :], lg[:, :, 0:NE], rows(gm[:, 0, :]), ALU.subtract
                                ).then_inc(S["ex_arg"], 1)
                assert link.n == LINKS["G"][0], ("G0", link.n)

            def router(b):
                link = Chain(ve, "linkG", sum(LINKS["G"]) * b + LINKS["G"][0])
                ve.wait_ge(S["ex_ready"], b + 1)
                link(V.tensor_reduce(gm[:, 1, :], pr[:, 0, :, :], AX.X, ALU.add))
                link(V.reciprocal(gm[:, 2, :], gm[:, 1, :]))
                link.mark(V.tensor_tensor(pr[:, 0, :, :], pr[:, 0, :, :], rows(gm[:, 2, :]), ALU.mult))
                link.wait()
                carrier()
                for t in range(TT):
                    link.mark(V.max(top[:, t, :], pr[:, 0, t, :]))
                link.wait()
                carrier()
                for t in range(TT):
                    link.mark(V.max_index(topi[:, t, :], top[:, t, :], pr[:, 0, t, :]))
                link.wait()
                link(V.tensor_copy(topf[:, 0, :, :], topi[:, :, 0:2]))
                link(V.tensor_tensor(gm[:, 4, :], top[:, :, 0], top[:, :, 1], ALU.add))
                link(V.reciprocal(gm[:, 5, :], gm[:, 4, :]))
                link(V.scalar_tensor_tensor(out=topf[:, 1, :, :], in0=top[:, :, 0:2], scalar=0.5,
                                            in1=gm[:, 5, :].rearrange("p (t o) -> p t o", o=1).broadcast_to([P, TT, 2]),
                                            op0=ALU.mult, op1=ALU.mult))
                for i in range(2):
                    link(V.tensor_tensor(pr[:, 1 + i, :, :],
                                         iota[:, :].rearrange("p (o e) -> p o e", o=1).broadcast_to([P, TT, NE]),
                                         rows(topf[:, 0, :, i]), ALU.is_equal))
                    link(V.tensor_tensor(pr[:, 1 + i, :, :], pr[:, 1 + i, :, :], rows(topf[:, 1, :, i]), ALU.mult))
                link(V.tensor_tensor(comb[:, :, 0:NE], pr[:, 1, :, :], pr[:, 2, :, :], ALU.add))
                link(V.tensor_scalar(gm[:, 3, :], gm[:, 3, :], 1.0, None, ALU.add))
                link(V.reciprocal(gm[:, 3, :], gm[:, 3, :]))
                V.tensor_scalar(comb[:, :, NE], gm[:, 3, :], 0.5, None, ALU.mult).then_inc(S["comb_ready"], 1)
                assert link.n == LINKS["G"][1], ("G1", link.n)

            head(0)
            stage_a(0, False)
            with ve.Fori(0, STEPS) as jj:
                step(0, jj, True, False)
            with ve.Fori(1, B) as b:
                head(b)
                residual(b - 1)
                stage_a(b, True)
                with ve.Fori(0, STEPS) as jj:
                    step(b, jj, True, True)
                finish(b - 1)
            residual(B - 1)
            whole_mlp(mlp_step, B - 1)
            with ve.Fori(0, STEPS) as jj:
                step(B, jj, False, True)
            finish(B - 1)

        @block.tensor
        def _(pe):
            mm = nc.tensor.matmul
            pe.wait_ge(S["const_in"], 16 * 7)
            pe.wait_ge(S["const_done"], 2)

            def norm_transposes(l, src, dst, xn_ready, done):
                for t in range(TT):
                    pe.wait_ge(S[xn_ready], TT * l + t + 1)
                    for k in range(KD):
                        ins = nc.tensor.transpose(dst[k][:, t * P:(t + 1) * P], src[:, t, k * P:(k + 1) * P], ident[:])
                ins.then_inc(S[done], 1)

            def head(b):
                norm_transposes(b, xn, bank[4:8], "a_xn_ready", "a_tr_done")

            def stage_a(b, mlp):
                pe.wait_ge(S["xT_ready"], KD * (b + 1))
                used = 0
                freed = []
                for kind, m in ITEMS:
                    freed.append({"xi": ("xpad_ready", NBLK * b + m + 1), "z": ("z_ready", NBLK * b + m + 1),
                                  "bc": ("bc_ready", b + 1), "dt": ("dt_ready", b + 1),
                                  "dl": ("relu_ready", NBLK * b + m + 1)}[kind])
                for n, (kind, m) in enumerate(ITEMS):
                    if mlp and n > 0:
                        mlp_steps(mlp_step, b - 1, n - 1, PE_BEHIND - 1)
                    ps = bank[4 + n % 4]
                    if n >= 4:
                        pe.wait_ge(S[freed[n - 4][0]], freed[n - 4][1])
                    if kind in ("xi", "z"):
                        pe.wait_ge(w_in_s[used % W_RING], 16 * (W_USES // W_RING * b + used // W_RING + 1))
                        for k in range(KD):
                            ins = mm(ps[:, :], wst[:, used % W_RING, k * P:(k + 1) * P], xT[:, k, :],
                                     start=(k == 0), stop=(k == KD - 1))
                        used += 1
                    elif kind == "bc":
                        pe.wait_ge(S["u_ready"], NBLK * (b + 1))
                        for k in range(NBLK):
                            ins = mm(ps[0:2 * NS, :], xpw[:, k, DTR:DTR + 2 * NS], u[:, k, :],
                                     start=(k == 0), stop=(k == NBLK - 1))
                    elif kind == "dt":
                        for k in range(NBLK):
                            ins = mm(ps[:, :], xpw[:, k, 0:DTR], u[:, k, :], start=(k == 0), stop=(k == NBLK - 1))
                    else:
                        pe.wait_ge(S["dt_ready"], b + 1)
                        ins = mm(ps[:, :], dtw[:, m * P:(m + 1) * P], dtT, start=True, stop=True)
                    ins.then_inc(S["a_ps"], 1)
                if mlp:
                    mlp_steps(mlp_step, b - 1, len(ITEMS) - 1, PE_BEHIND - 1)
                pe.wait_ge(S["z_ready"], NBLK * (b + 1))

            def step(b, jj, scan, experts):
                q = STEPS * b + jj
                qe = STEPS * (b - 1) + jj

                def nsum(c):
                    jl, s = c // CHUNKS, c % 4
                    first, last = c % CHUNKS == (1 if experts else 0), c % CHUNKS == CHUNKS - 1
                    if first:
                        pe.wait_ge(S["y_done"], 2 + BLK_Q * q + jl - 1)
                    if experts:
                        if c // 2 < QUADS_P:
                            pe.wait_ge(S["quad_ready"], QUADS_P * (q - STEPS) + c // 2 + 1)
                        else:
                            pe.wait_ge(S["quad_v_ready"], QUADS_V * (q - STEPS) + c // 2 - QUADS_P + 1)
                        mm(Y[jl % 2][:, :], ident[:], pairs[:, s - 1, :], start=first, stop=last
                           ).then_inc(S["nsum_done"], 1)
                    else:
                        pe.wait_ge(S["prod_done"], CH_Q * q + c + 1)
                        mm(Y[jl % 2][:, :], ident[:], dBu[:, s, 0, :], start=first, stop=False)
                        mm(Y[jl % 2][:, :], ident[:], dBu[:, s, 1, :], start=False, stop=last
                           ).then_inc(S["hs_ready"], 1)

                def phase(kind, i):
                    sl = i % SLOTS_E
                    if kind == "g":
                        pe.wait_ge(ew_up[sl], 16 * (EXP_Q // SLOTS_E * qe + i // SLOTS_E + 1))
                        pe.wait_ge(S["t1_done"], ONE + EXP_Q * qe + i)
                    if kind == "u":
                        pe.wait_ge(S["t2_done"], ONE + EXP_Q * qe + i)
                    if kind in "gu":
                        o = 0 if kind == "g" else D
                        for k in range(KD):
                            ins = mm((G if kind == "g" else U)[:, :], ew[:, sl, o + k * P:o + (k + 1) * P], x3T[:, k, :],
                                     start=(k == 0), stop=(k == KD - 1))
                        ins.then_inc(S["g_done" if kind == "g" else "u_done"], 1)
                    else:
                        pe.wait_ge(S["hm_ready"], ONE + EXP_Q * qe + i + 1)
                        pe.wait_ge(ew_down[sl], 32 * (EXP_Q // SLOTS_E * qe + i // SLOTS_E + 1))
                        for t in range(TT):
                            ins = mm(acc[t][:, :], hm[:, i % 2, t * P:(t + 1) * P], ew[:, sl, 2 * D:3 * D],
                                     start=False, stop=False, skip_group_check=True)
                        ins.then_inc(S["down_done"], 1)

                for p in range(CH_Q + NSUM_BEHIND):
                    if experts and p < len(PHASES):
                        phase(*PHASES[p])
                    c = p - NSUM_BEHIND
                    if scan and c >= 0 and (not experts or c % 2 == 1):
                        nsum(c)

            def experts_begin(b):
                pe.wait_ge(S["x3_ready"], KD * b)
                pe.wait_ge(S["cT_ready"], b)
                for t in range(TT):
                    mm(acc[t][:, :], zerob[:], zeros4,
                       start=True, stop=False, skip_group_check=True)

            def experts_end():
                for t in range(TT):
                    ins = mm(acc[t][:, :], zerob[:], zeros4, start=False, stop=True, skip_group_check=True)
                ins.then_inc(S["moe_done"], 1)

            zeros4 = zerob[:, 0:P].rearrange("p (o c) -> p o c", o=1).broadcast_to([P, 4, P])

            def mlp_step(b, k):
                layer = int(k[-1]) if k[-1] in "01" else 0
                r, kt = 2 * b + layer, (KD, 2)[layer]
                if k in ("norm0", "norm1"):
                    norm_transposes(2 * b + layer, x1n, acc, "xn_ready", "tr_done")
                elif k in ("diag0", "diag1"):
                    pe.wait_ge(S["diag_ready"], 2 * (KD + 2) * b + (2 * (KD + 2) if layer else 2 * KD))
                    for dst, d0 in ((acc[0], 0), (acc[1], 4)):
                        for i in range(kt):
                            ins = mm(dst[:, i * P:(i + 1) * P], ones[:], dg[:, d0 + i, :], start=True, stop=True)
                    ins.then_inc(S["sbc_ps"], 1)
                elif k in ("scales0", "scales1"):
                    pe.wait_ge(S["wdiag_ready"], TT * (r + 1))
                    for i in range(TT):
                        ins = mm(acc[2][:, i * P:(i + 1) * P], ones[:], dg[:, i, :], start=True, stop=True)
                    ins.then_inc(S["wsc_ps"], 1)
                elif k in ("integers0", "integers1"):
                    width = kt * P
                    for i in range(2):
                        if i == 1:
                            pe.wait_ge(S["wsc_ready"], r + 1)
                        for t in range(TT):
                            pe.wait_ge(S["q_ready"], 2 * TT * r + TT * i + t + 1)
                            for f in range(kt):
                                o = (f % 2) * T + t * P
                                ins = nc.tensor.transpose(accb[2 * i + f // 2][:, o:o + P],
                                                          q_rows[i][:, t * width + f * P:t * width + (f + 1) * P],
                                                          identb[:])
                        ins.then_inc(S["qT_ps"], 1)
                elif k in ("transposed0", "transposed1"):
                    pe.wait_ge(S["qT_ready"], 2 * r + 2)
                    for t in range(TT):
                        for f in range(kt):
                            ins = mm(acc[t][:, :], q_cols[0][:, f * T + t * P:f * T + (t + 1) * P],
                                     q_cols[1][:, f * T:(f + 1) * T], start=(f == 0), stop=(f == kt - 1))
                        ins.then_inc(S["lin_ps"], 1)
                elif k == "act":
                    for t in range(TT):
                        pe.wait_ge(S["a_ready"], TT * b + t + 1)
                        for f in range(INT // P):
                            ins = nc.tensor.transpose(acc[f][:, t * P:(t + 1) * P], act[:, t, f * P:(f + 1) * P],
                                                      ident[:])
                    ins.then_inc(S["xc_ps"], 1)
                elif k == "x3":
                    pe.wait_ge(S["x3_ready"], KD * (b + 1))
                    for t in range(TT):
                        for f in range(KD):
                            ins = mm(acc[0][:, t * (NE + 1):(t + 1) * (NE + 1)], x3T[:, f, t * P:(t + 1) * P],
                                     gatew[:, f, :], start=(f == 0), stop=(f == KD - 1))
                    ins.then_inc(S["lg_ps"], 1)
                elif k == "router":
                    pe.wait_ge(S["comb_ready"], b + 1)
                    for t in range(TT):
                        ins = nc.tensor.transpose(acc[1][0:NE + 1, t * P:(t + 1) * P], comb[:, t, :], ident[:])
                    ins.then_inc(S["comb_ps"], 1)

            def mixer_out(b, ks):
                pe.wait_ge(S["fin_done"], ONE + TT * b)
                pe.wait_ge(S["y_done"], 2 + NBLK * (b + 1))
                for k in ks:
                    n = len(W_ITEMS) + k
                    pe.wait_ge(w_in_s[n % W_RING], 16 * (W_USES // W_RING * b + n // W_RING + 1))
                    for t in range(TT):
                        ins = mm(acc[t][:, :], zg[:, k, t * P:(t + 1) * P], wst[:, n % W_RING, :],
                                 start=(k == 0), stop=(k == NBLK - 1))
                    ins.then_inc(S["o_used"], 1)

            head(0)
            stage_a(0, False)
            with pe.Fori(0, STEPS) as jj:
                step(0, jj, True, False)
            with pe.Fori(1, B) as b:
                mixer_out(b - 1, range(NBLK // 2))
                head(b)
                mixer_out(b - 1, range(NBLK // 2, NBLK))
                stage_a(b, True)
                experts_begin(b)
                with pe.Fori(0, STEPS) as jj:
                    step(b, jj, True, True)
                experts_end()
            mixer_out(B - 1, range(NBLK))
            whole_mlp(mlp_step, B - 1)
            experts_begin(B)
            with pe.Fori(0, STEPS) as jj:
                step(B, jj, False, True)
            experts_end()


def kernel(**a):
    import concourse.bacc as bacc
    from concourse.bass_utils import run_bass_kernel_spmd as run

    a = {k: np.asarray(v) for k, v in a.items()}

    def blocks(w, rows):
        o, i = w.shape
        return np.ascontiguousarray(w.reshape(o // rows, rows, i // P, P).transpose(0, 3, 2, 1)).reshape(
            o // rows, P, (i // P) * rows)

    def cols(w):
        o, i = w.shape
        return np.ascontiguousarray(w.reshape(o, i // P, P).transpose(2, 1, 0))

    def tiles(v):
        return np.ascontiguousarray(v.reshape(v.shape[0] // P, P, -1).transpose(1, 0, 2))

    gu, dn = a["fside_BxS2xS2_0"], a["ctx_1024"]
    w1 = np.concatenate([a["L0_ffn_w1"], a["L0_ffn_ws_gate"].reshape(NSH, P, D)])
    w3 = np.concatenate([a["L0_ffn_w3"], a["L0_ffn_ws_up"].reshape(NSH, P, D)])
    w2 = np.concatenate([a["L0_ffn_w2"], a["L0_ffn_ws_down"].reshape(D, NSH, P).transpose(1, 0, 2)])
    up = [np.concatenate([blocks(w, P)[0] for w in ws])[None].reshape(NE + NSH, P, D) for ws in (w1, w3)]
    arrays = {
        "x": a["x"],
        "w_in": blocks(a["L0_attn_in_proj_weight"], P),
        "conv_w": tiles(a["L0_attn_conv1d_weight"].reshape(DI, TAPS)),
        "xp_w": cols(a["L0_attn_x_proj_weight"]),
        "dt_w": np.ascontiguousarray(a["L0_attn_dt_proj_weight"].T),
        "dt_b": tiles(a["L0_attn_dt_proj_bias"]).reshape(P, NBLK),
        "a_log": tiles(a["L0_attn_A_log"]),
        "d_skip": tiles(a["L0_attn_D"]).reshape(P, NBLK),
        "out_w": np.ascontiguousarray(a["L0_attn_out_proj_weight"].T).reshape(NBLK, P, D),
        "gu_w": np.stack([tiles(w) for w in gu]),
        "gu_wT": np.stack([cols(w) for w in gu]),
        "dn_w": np.stack([tiles(w) for w in dn]),
        "dn_wT": np.stack([cols(w) for w in dn]),
        "gate_w": cols(np.concatenate([a["L0_ffn_gate_w"], a["L0_ffn_shared_gate_w"]])),
        "exp_w": np.concatenate([up[0], up[1], np.ascontiguousarray(w2.transpose(0, 2, 1))], axis=2),
    }
    nc = bacc.Bacc("TRN2", target_bir_lowering=False, num_devices=1)
    args = {}
    for name, v in arrays.items():
        arrays[name] = np.ascontiguousarray(v)
        args[name] = nc.dram_tensor(f"in_{name}", v.shape, F32, kind="ExternalInput").ap()
    out = nc.dram_tensor("out_0", (B, T, D), F32, kind="ExternalOutput").ap()
    build(nc, out=out, **args)
    r = run(nc, [{f"in_{k}": v for k, v in arrays.items()}], core_ids=[0])
    return r.results[0]["out_0"]
```
